# Optimizing a Trainium2 kernel written in Bass

```python
import numpy as np
import jax
import jax.numpy as jnp

def _softmax(x, axis=-1):
    return jax.nn.softmax(x, axis=axis)

def _gelu(x):
    return jax.nn.gelu(x, approximate=True)

def _silu(x):
    return jax.nn.silu(x)

def _sigmoid(x):
    return jax.nn.sigmoid(x)

def _layernorm(x, axis=-1, eps=1e-05):
    m = jnp.mean(x, axis=axis, keepdims=True)
    v = jnp.var(x, axis=axis, keepdims=True)
    return (x - m) / jnp.sqrt(v + eps)

def _scatter_add(tgt, idx, src, axis=0):
    return tgt.at[idx].add(src)

def _segment_sum(src, seg, n):
    return jax.ops.segment_sum(src, seg, n)
kernel_name = 'mk_gnn_resnorm_d2_gnn_r32_3a46ba'

def setup_inputs(seed: int=0):
    np.random.seed(seed)
    _w = jnp.asarray

    def _rec_inputs():
        import jax
        import jax.numpy as jnp
        _gk = jax.random.key(seed)
        x = -0.000202 + 1 * jax.random.normal(jax.random.fold_in(_gk, 1), (50000, 160), jnp.float32)
        src = jax.random.randint(jax.random.fold_in(_gk, 2), (25000,), 0, 50000, jnp.int32)
        dst = jax.random.randint(jax.random.fold_in(_gk, 3), (25000,), 0, 50000, jnp.int32)
        _o = jnp.argsort(dst, stable=True)
        src = src[_o]
        dst = dst[_o]
        edge_attr_16 = -0.000191324 + 0.999809 * jax.random.normal(jax.random.fold_in(_gk, 12), (25000, 16), jnp.float32)
        edge_attr_4 = 0.0012443 + 1.0001 * jax.random.normal(jax.random.fold_in(_gk, 13), (25000, 4), jnp.float32)
        edge_attr_64 = 0.000127647 + 1.00004 * jax.random.normal(jax.random.fold_in(_gk, 14), (25000, 64), jnp.float32)
        node_vec1 = jax.random.uniform(jax.random.fold_in(_gk, 15), (50000, 1), jnp.float32, 0.0, 1)
        return (x, src, dst, edge_attr_16, edge_attr_4, edge_attr_64, node_vec1)
    x, src, dst, edge_attr_16, edge_attr_4, edge_attr_64, node_vec1 = _rec_inputs()

    def _L0_gnn_setup():
        import jax, jax.numpy as jnp
        import numpy as np
        N, E = (1250, 20000)
        S_IN, V_IN = (64, 32)
        S_MID, V_MID = (96, 128)
        S_OUT, V_OUT = (96, 32)
        R = 64
        FC_HID = 64
        W_NUMEL = 64 + 64 + 32 + 32 + 32
        NUM_NEIGHBORS = 16.0

        def _inv(d):
            return 1.0 / jnp.sqrt(jnp.float32(d))

        def _forward(node_features, node_attr, edge_attr, edge_scalars, lin1_ws, lin1_wv, fc_w1, fc_w2, sc_ws, sc_wv, lin2_ws, lin2_wv, edge_src, edge_dst):
            n = node_features.shape[0]
            s = node_features[:, :S_IN]
            v = node_features[:, S_IN:].reshape(n, V_IN, 3)
            a = node_attr
            sc_s = s @ sc_ws * a * _inv(S_IN)
            sc_v = jnp.einsum('nci,cd->ndi', v, sc_wv) * a[:, :, None] * _inv(V_IN)
            h_s = s @ lin1_ws * a * _inv(S_IN)
            h_v = jnp.einsum('nci,cd->ndi', v, lin1_wv) * a[:, :, None] * _inv(V_IN)
            hid = jax.nn.silu(edge_scalars @ fc_w1 * _inv(R))
            w = hid @ fc_w2 * _inv(FC_HID)
            w1, w2, w3, w4, w5 = jnp.split(w, [64, 128, 160, 192], axis=-1)
            es = h_s[edge_src]
            ev = h_v[edge_src]
            e0 = edge_attr[:, :1]
            e1 = edge_attr[:, 1:4]
            m_s1 = w1 * es * e0
            m_s2 = w4 * jnp.einsum('eci,ei->ec', ev, e1) * _inv(3)
            m_v1 = (w2 * es)[:, :, None] * e1[:, None, :]
            m_v2 = w3[:, :, None] * ev * e0[:, :, None]
            m_v3 = w5[:, :, None] * jnp.cross(ev, e1[:, None, :]) * _inv(2)
            mid_s = jnp.concatenate([m_s1, m_s2], axis=-1)
            mid_v = jnp.concatenate([m_v1, m_v2, m_v3], axis=1)
            inv_nn = 1.0 / jnp.sqrt(jnp.float32(NUM_NEIGHBORS))
            agg_s = jax.ops.segment_sum(mid_s, edge_dst, num_segments=n) * inv_nn
            agg_v = jax.ops.segment_sum(mid_v, edge_dst, num_segments=n) * inv_nn
            o_s = agg_s @ lin2_ws * a * _inv(S_MID)
            o_v = jnp.einsum('nci,cd->ndi', agg_v, lin2_wv) * a[:, :, None] * _inv(V_MID)
            pre_s = sc_s + o_s
            pre_v = sc_v + o_v
            scalars = jax.nn.silu(pre_s[:, :64])
            gates = jax.nn.sigmoid(pre_s[:, 64:96])
            gated = gates[:, :, None] * pre_v
            return jnp.concatenate([scalars, gated.reshape(n, 3 * V_OUT)], axis=-1)
        key = jax.random.key(seed)
        ks = jax.random.split(key, 13)
        return {'node_features': jax.random.normal(ks[0], (N, S_IN + 3 * V_IN), jnp.float32), 'node_attr': jnp.ones((N, 1), jnp.float32), 'edge_src': jax.random.randint(ks[1], (E,), 0, N), 'edge_dst': jax.random.randint(ks[2], (E,), 0, N), 'edge_attr': jax.random.normal(ks[3], (E, 4), jnp.float32), 'edge_scalars': jax.random.normal(ks[4], (E, R), jnp.float32), 'lin1_ws': jax.random.normal(ks[5], (S_IN, S_IN), jnp.float32), 'lin1_wv': jax.random.normal(ks[6], (V_IN, V_IN), jnp.float32), 'fc_w1': jax.random.normal(ks[7], (R, FC_HID), jnp.float32), 'fc_w2': jax.random.normal(ks[8], (FC_HID, W_NUMEL), jnp.float32), 'sc_ws': jax.random.normal(ks[9], (S_IN, S_OUT), jnp.float32), 'sc_wv': jax.random.normal(ks[10], (V_IN, V_OUT), jnp.float32), 'lin2_ws': jax.random.normal(ks[11], (S_MID, S_OUT), jnp.float32), 'lin2_wv': jax.random.normal(ks[12], (V_MID, V_OUT), jnp.float32)}
    _L0_gnn_all = _L0_gnn_setup()
    _L0_gnn_in = {k: v for k, v in _L0_gnn_all.items() if k in ('lin1_ws', 'lin1_wv', 'fc_w1', 'fc_w2', 'sc_ws', 'sc_wv', 'lin2_ws', 'lin2_wv')}
    del _L0_gnn_all

    def _L1_gnn_setup():
        import jax, jax.numpy as jnp
        import numpy as np
        N = 625
        E = 10000
        MUL0 = 64
        MUL1 = 32
        FC_IN = 16
        FC_H = 64
        WNUM = 192
        key = jax.random.key(seed)
        ks = jax.random.split(key, 16)
        return {'x': jax.random.normal(ks[0], (N, MUL0 + 3 * MUL1), jnp.float32), 'node_attr': jnp.ones((N, 1), jnp.float32), 'edge_scalars': jax.random.normal(ks[1], (E, FC_IN), jnp.float32), 'edge_attr_sh': jax.random.normal(ks[2], (E, 4), jnp.float32), 'edge_src': jax.random.randint(ks[3], (E,), 0, N), 'edge_dst': jax.random.randint(ks[4], (E,), 0, N), 'Wfc1': jax.random.normal(ks[5], (FC_IN, FC_H), jnp.float32), 'Wfc2': jax.random.normal(ks[6], (FC_H, WNUM), jnp.float32), 'Wsc0': jax.random.normal(ks[7], (MUL0, MUL0), jnp.float32), 'Wsc1': jax.random.normal(ks[8], (MUL1, MUL1), jnp.float32), 'Wl1_0': jax.random.normal(ks[9], (MUL0, MUL0), jnp.float32), 'Wl1_1': jax.random.normal(ks[10], (MUL1, MUL1), jnp.float32), 'Wl2_s': jax.random.normal(ks[11], (MUL0 + MUL1, MUL0), jnp.float32), 'Wl2_v': jax.random.normal(ks[12], (MUL0 + MUL1, MUL1), jnp.float32), 'Wa': 0.1 * jax.random.normal(ks[13], (MUL0 + MUL1, 1), jnp.float32)}
    _L1_gnn_all = _L1_gnn_setup()
    _L1_gnn_in = {k: v for k, v in _L1_gnn_all.items() if k in ('Wfc1', 'Wfc2', 'Wsc0', 'Wsc1', 'Wl1_0', 'Wl1_1', 'Wl2_s', 'Wl2_v', 'Wa')}
    del _L1_gnn_all
    return {'x': x, 'src': src, 'dst': dst, 'edge_attr_16': edge_attr_16, 'edge_attr_4': edge_attr_4, 'edge_attr_64': edge_attr_64, 'node_vec1': node_vec1, 'L0_gnn_lin1_ws': _L0_gnn_in['lin1_ws'], 'L0_gnn_lin1_wv': _L0_gnn_in['lin1_wv'], 'L0_gnn_fc_w1': _L0_gnn_in['fc_w1'], 'L0_gnn_fc_w2': _L0_gnn_in['fc_w2'], 'L0_gnn_sc_ws': _L0_gnn_in['sc_ws'], 'L0_gnn_sc_wv': _L0_gnn_in['sc_wv'], 'L0_gnn_lin2_ws': _L0_gnn_in['lin2_ws'], 'L0_gnn_lin2_wv': _L0_gnn_in['lin2_wv'], 'L1_gnn_Wfc1': _L1_gnn_in['Wfc1'], 'L1_gnn_Wfc2': _L1_gnn_in['Wfc2'], 'L1_gnn_Wsc0': _L1_gnn_in['Wsc0'], 'L1_gnn_Wsc1': _L1_gnn_in['Wsc1'], 'L1_gnn_Wl1_0': _L1_gnn_in['Wl1_0'], 'L1_gnn_Wl1_1': _L1_gnn_in['Wl1_1'], 'L1_gnn_Wl2_s': _L1_gnn_in['Wl2_s'], 'L1_gnn_Wl2_v': _L1_gnn_in['Wl2_v'], 'L1_gnn_Wa': _L1_gnn_in['Wa']}

def reference(x, src, dst, edge_attr_16, edge_attr_4, edge_attr_64, node_vec1, L0_gnn_lin1_ws, L0_gnn_lin1_wv, L0_gnn_fc_w1, L0_gnn_fc_w2, L0_gnn_sc_ws, L0_gnn_sc_wv, L0_gnn_lin2_ws, L0_gnn_lin2_wv, L1_gnn_Wfc1, L1_gnn_Wfc2, L1_gnn_Wsc0, L1_gnn_Wsc1, L1_gnn_Wl1_0, L1_gnn_Wl1_1, L1_gnn_Wl2_s, L1_gnn_Wl2_v, L1_gnn_Wa):
    import jax
    import jax.numpy as jnp

    def _L0_gnn_ref(node_features, node_attr, edge_src, edge_dst, edge_attr, edge_scalars, lin1_ws, lin1_wv, fc_w1, fc_w2, sc_ws, sc_wv, lin2_ws, lin2_wv):
        import jax, jax.numpy as jnp
        import numpy as np
        N, E = (1250, 20000)
        S_IN, V_IN = (64, 32)
        S_MID, V_MID = (96, 128)
        S_OUT, V_OUT = (96, 32)
        R = 64
        FC_HID = 64
        W_NUMEL = 64 + 64 + 32 + 32 + 32
        NUM_NEIGHBORS = 16.0

        def _inv(d):
            return 1.0 / jnp.sqrt(jnp.float32(d))

        def _forward(node_features, node_attr, edge_attr, edge_scalars, lin1_ws, lin1_wv, fc_w1, fc_w2, sc_ws, sc_wv, lin2_ws, lin2_wv, edge_src, edge_dst):
            n = node_features.shape[0]
            s = node_features[:, :S_IN]
            v = node_features[:, S_IN:].reshape(n, V_IN, 3)
            a = node_attr
            sc_s = s @ sc_ws * a * _inv(S_IN)
            sc_v = jnp.einsum('nci,cd->ndi', v, sc_wv) * a[:, :, None] * _inv(V_IN)
            h_s = s @ lin1_ws * a * _inv(S_IN)
            h_v = jnp.einsum('nci,cd->ndi', v, lin1_wv) * a[:, :, None] * _inv(V_IN)
            hid = jax.nn.silu(edge_scalars @ fc_w1 * _inv(R))
            w = hid @ fc_w2 * _inv(FC_HID)
            w1, w2, w3, w4, w5 = jnp.split(w, [64, 128, 160, 192], axis=-1)
            es = h_s[edge_src]
            ev = h_v[edge_src]
            e0 = edge_attr[:, :1]
            e1 = edge_attr[:, 1:4]
            m_s1 = w1 * es * e0
            m_s2 = w4 * jnp.einsum('eci,ei->ec', ev, e1) * _inv(3)
            m_v1 = (w2 * es)[:, :, None] * e1[:, None, :]
            m_v2 = w3[:, :, None] * ev * e0[:, :, None]
            m_v3 = w5[:, :, None] * jnp.cross(ev, e1[:, None, :]) * _inv(2)
            mid_s = jnp.concatenate([m_s1, m_s2], axis=-1)
            mid_v = jnp.concatenate([m_v1, m_v2, m_v3], axis=1)
            inv_nn = 1.0 / jnp.sqrt(jnp.float32(NUM_NEIGHBORS))
            agg_s = jax.ops.segment_sum(mid_s, edge_dst, num_segments=n) * inv_nn
            agg_v = jax.ops.segment_sum(mid_v, edge_dst, num_segments=n) * inv_nn
            o_s = agg_s @ lin2_ws * a * _inv(S_MID)
            o_v = jnp.einsum('nci,cd->ndi', agg_v, lin2_wv) * a[:, :, None] * _inv(V_MID)
            pre_s = sc_s + o_s
            pre_v = sc_v + o_v
            scalars = jax.nn.silu(pre_s[:, :64])
            gates = jax.nn.sigmoid(pre_s[:, 64:96])
            gated = gates[:, :, None] * pre_v
            return jnp.concatenate([scalars, gated.reshape(n, 3 * V_OUT)], axis=-1)
        return _forward(node_features, node_attr, edge_attr, edge_scalars, lin1_ws, lin1_wv, fc_w1, fc_w2, sc_ws, sc_wv, lin2_ws, lin2_wv, edge_src, edge_dst)

    def _L1_gnn_ref(x, node_attr, edge_scalars, edge_attr_sh, edge_src, edge_dst, Wfc1, Wfc2, Wsc0, Wsc1, Wl1_0, Wl1_1, Wl2_s, Wl2_v, Wa):
        import jax, jax.numpy as jnp
        import numpy as np
        N = 625
        E = 10000
        MUL0 = 64
        MUL1 = 32
        FC_IN = 16
        FC_H = 64
        WNUM = 192
        n = x.shape[0]
        x0 = x[:, :MUL0]
        x1 = x[:, MUL0:].reshape(n, MUL1, 3)
        a = node_attr
        h = jax.nn.silu(edge_scalars @ (Wfc1 / jnp.sqrt(jnp.float32(FC_IN))))
        w = h @ (Wfc2 / jnp.sqrt(jnp.float32(FC_H)))
        w0 = w[:, :64]
        w1 = w[:, 64:128]
        w2 = w[:, 128:160]
        w3 = w[:, 160:192]
        inv8 = 1.0 / jnp.sqrt(jnp.float32(MUL0))
        inv32 = 1.0 / jnp.sqrt(jnp.float32(MUL1))
        sc = jnp.concatenate([x0 @ Wsc0 * a * inv8, (jnp.einsum('num,uv->nvm', x1, Wsc1) * a[..., None] * inv32).reshape(n, 3 * MUL1)], axis=1)
        f0 = x0 @ Wl1_0 * a * inv8
        f1 = jnp.einsum('num,uv->nvm', x1, Wl1_1) * a[..., None] * inv32
        e0 = f0[edge_src]
        e1 = f1[edge_src]
        sh0 = edge_attr_sh[:, :1]
        sh1 = edge_attr_sh[:, 1:4]
        mid0 = w0 * e0 * sh0
        mid1 = w3 * jnp.einsum('eum,em->eu', e1, sh1) / jnp.sqrt(3.0)
        mid2 = w1[:, :, None] * e0[:, :, None] * sh1[:, None, :]
        mid3 = w2[:, :, None] * e1 * sh0[:, :, None]
        cnt = jnp.clip(jax.ops.segment_sum(jnp.ones(edge_dst.shape, x.dtype), edge_dst, num_segments=n), 1.0)

        def smean(v):
            s = jax.ops.segment_sum(v, edge_dst, num_segments=n)
            return s / cnt.reshape((n,) + (1,) * (v.ndim - 1))
        n0, n1 = (smean(mid0), smean(mid1))
        n2, n3 = (smean(mid2), smean(mid3))
        scal = jnp.concatenate([n0, n1], axis=1)
        vec = jnp.concatenate([n2, n3], axis=1)
        inv96 = 1.0 / jnp.sqrt(jnp.float32(MUL0 + MUL1))
        alpha = scal @ Wa * a * inv96
        out_s = scal @ Wl2_s * a * inv96
        out_v = jnp.einsum('num,uv->nvm', vec, Wl2_v) * a[..., None] * inv96
        conv = jnp.concatenate([out_s, out_v.reshape(n, 3 * MUL1)], axis=1)
        return sc + alpha * conv
    x = _layernorm(x + _L0_gnn_ref(x, node_vec1, src, dst, edge_attr_4, edge_attr_64, L0_gnn_lin1_ws, L0_gnn_lin1_wv, L0_gnn_fc_w1, L0_gnn_fc_w2, L0_gnn_sc_ws, L0_gnn_sc_wv, L0_gnn_lin2_ws, L0_gnn_lin2_wv), axis=-1)
    x = _layernorm(x + _L1_gnn_ref(x, node_vec1, edge_attr_16, edge_attr_4, src, dst, L1_gnn_Wfc1, L1_gnn_Wfc2, L1_gnn_Wsc0, L1_gnn_Wsc1, L1_gnn_Wl1_0, L1_gnn_Wl1_1, L1_gnn_Wl2_s, L1_gnn_Wl2_v, L1_gnn_Wa), axis=-1)
    return x

_drawn_inputs = setup_inputs


def setup_inputs(seed=0):
    import zlib

    import numpy as np

    out = dict(_drawn_inputs(seed))
    spreads = {}
    factors = {'edge_attr_16': 8.0,
     'edge_attr_4': 3.036,
     'edge_attr_64': 3.385,
     'L0_gnn_lin1_ws': 4.077,
     'L0_gnn_lin1_wv': 4.765,
     'L0_gnn_fc_w1': 3.394,
     'L0_gnn_fc_w2': 3.194,
     'L0_gnn_lin2_ws': 4.682,
     'L0_gnn_lin2_wv': 4.319,
     'L1_gnn_Wfc1': 8.0,
     'L1_gnn_Wfc2': 8.0,
     'L1_gnn_Wl1_0': 8.0,
     'L1_gnn_Wl1_1': 8.0,
     'L1_gnn_Wl2_s': 8.0,
     'L1_gnn_Wl2_v': 8.0,
     'L1_gnn_Wa': 8.0}
    for name, (base, spread) in spreads.items():
        noise = np.random.default_rng([zlib.crc32(name.encode()), seed]).standard_normal(out[name].shape)
        drawn = base * np.exp(spread * noise) if base else spread * noise
        out[name] = jnp.asarray(drawn.astype(out[name].dtype))
    for name, factor in factors.items():
        out[name] = (out[name] * factor).astype(out[name].dtype)
    return out
```

```python
import math

import numpy as np
import concourse.bass as bass
from concourse import mybir
from contextlib import ExitStack

F32 = mybir.dt.float32
I32 = mybir.dt.int32
ALU = mybir.AluOpType
ACT = mybir.ActivationFunctionType

P = 128
N, E = 50000, 25000
S, V = 64, 32
D = S + 3 * V
PAIR = 2 * P
NP = -(-E // PAIR)
T = 4
GROUP = T * P
NG = -(-N // GROUP)
N_PAD = NG * GROUP
ROWS = N_PAD + PAIR
H = 64
EPS = 1e-5

LAYERS = [
    dict(R=64, W=224, SO=96, SG=96, ROW=192, cross=True),
    dict(R=16, W=192, SO=65, SG=64, ROW=162, cross=False),
]


def wait_count(eng, sem, n):
    if not isinstance(n, int) or n > 0:
        eng.wait_ge(sem, n)


def run_stages(eng, base, count, depth, stages):
    for k in range(base, base + depth):
        for lag, f in stages:
            if k - lag >= base:
                f(k - lag, k - lag - base, (k - lag) % 2)
    with eng.Fori(base + depth, base + count - 1, 2) as i:
        for u in range(2):
            for lag, f in stages:
                f(i + (u - lag), i + (u - lag - base), (u - lag) % 2)
    for k in range(base + count, base + count + depth):
        for lag, f in stages:
            if k - lag < base + count:
                f(k - lag, k - lag - base, (k - lag) % 2)


def program(nc, A, out):
    ctx = ExitStack()
    with ctx:
        def sb(name, shape, dt=F32):
            return ctx.enter_context(nc.sbuf_tensor(name, shape, dt))

        def two(name, shape, dt=F32):
            return [sb(f"{name}{u}", shape, dt) for u in range(2)]

        def sem(name):
            return ctx.enter_context(nc.semaphore(name))

        def sem2(name):
            return [sem(f"{name}{u}") for u in range(2)]

        def dram(name, shape):
            return nc.dram_tensor(name, shape, F32, kind="Internal").ap()

        x1_rows = dram("x1_rows", (N_PAD, D))
        table = [dram(f"table{l}", (ROWS, LAYERS[l]["ROW"])) for l in range(2)]

        ident = sb("ident", [P, P])
        fc1 = [sb("fc1_0", [P, 2 * H]), sb("fc1_1", [32, 2 * H])]
        fc2 = [sb(f"fc2_{l}", [P, LAYERS[l]["W"]]) for l in range(2)]
        lin1_s = [sb(f"lin1_s{l}", [S, S]) for l in range(2)]
        lin1_v = [sb(f"lin1_v{l}", [3 * V, 3 * V]) for l in range(2)]
        mapA = [sb(f"mapA{l}", [P, LAYERS[l]["SO"] + V]) for l in range(2)]
        mapB = [sb(f"mapB{l}", [P, 3 * V]) for l in range(2)]
        mapC = sb("mapC", [3 * V, 3 * V])
        self_s = [sb(f"self_s{l}", [S, LAYERS[l]["SG"]]) for l in range(2)]
        self_v = [sb(f"self_v{l}", [3 * V, 3 * V]) for l in range(2)]
        zeros = sb("zeros", [P, 16 * 192])
        earlier = sb("earlier", [P, P])
        spare_row = sb("spare_row", [P, 2])
        spare_i = sb("spare_i", [P, 2], I32)
        minus_half = sb("minus_half", [P, T])
        quarter = sb("quarter", [P, T])

        dst_all = sb("dst_all", [P, NP * 2], I32)
        attr_all = sb("attr_all", [P, NP * 2, 6])
        ea_all = sb("ea_all", [P, NP * 2, 6])
        row_all = sb("row_all", [P, NP * 2], I32)

        src_i = two("src_i", [P, 2], I32)
        xg = two("xg", [P, 2, D + 1])
        attrT = two("attrT", [P, P])
        dst_row = two("dst_row", [P, PAIR], I32)
        xgT = two("xgT", [P, 4, P])
        hidT = two("hidT", [P, P])
        hs = two("hs", [P, 2, D + 2 * V])
        ea = two("ea", [P, 2, 6])
        mid = two("mid", [P, 2, 352])
        midT = two("midT", [P, 6, P])
        msg = [two(f"msg{l}_", [P, 2, LAYERS[l]["ROW"]]) for l in range(2)]
        pe1 = two("pe1", [P, 2, 3 * V])
        same0 = two("same0", [P, P])
        same1 = two("same1", [P, PAIR])
        sums = two("sums", [P, 2, 192])
        row_i = two("row_i", [P, 2], I32)
        prod = sb("prod", [P, 2, 3 * V])
        crossA = sb("crossA", [P, 2, 3 * V])
        crossB = sb("crossB", [P, 2, 3 * V])
        dot = sb("dot", [P, 2, V])
        dst_f = sb("dst_f", [P, 2])
        to_spare = sb("to_spare", [P, 2])
        n_before = sb("n_before", [P, 3])
        later = sb("later", [P, 2])
        junk = sb("junk", [P, PAIR])

        xsT = two("xsT", [S, GROUP])
        xvT = two("xvT", [3 * V, GROUP])
        x1g = two("x1g", [P, T, D])
        tab = two("tab", [P, T, 192])
        a_n = two("a_n", [P, T])
        pre = two("pre", [P, T, 192])
        gate = two("gate", [P, T, 96])
        res = two("res", [P, T, D])
        stats = two("stats", [P, T, 6])
        mean2, apart, squares, apart2, var_in, var_e, neg_mean = [
            sb(n, [P, T]) for n in ("mean2", "apart", "squares", "apart2", "var_in", "var_e", "neg_mean")]
        rstd = two("rstd", [P, T])
        shift = two("shift", [P, T])
        y = two("y", [P, T, D])
        small = two("small", [P, T, 4])

        ps = ctx.enter_context(nc.psum_tensor("ps", [P, 8 * 512], F32))

        def bank(b, n=512):
            return ps[:, b * 512:b * 512 + n]

        xgT_ps = bank(0).rearrange("p (k e) -> p k e", k=4)
        hidT_ps = bank(1)[:, 384:512]
        h_ps = bank(1, 2 * D).rearrange("p (t c) -> p t c", t=2)
        w_ps = [ps[:, 1024:2048].rearrange("p (t c) -> p t c", t=2)[:, :, 0:L["W"]] for L in LAYERS]
        midT_ps = bank(4, 768).rearrange("p (k e) -> p k e", k=6)
        o_ps = [bank(6, 2 * (L["SO"] + 128)).rearrange("p (t c) -> p t c", t=2) for L in LAYERS]
        sum_ps = [bank(7, 2 * L["ROW"]).rearrange("p (t c) -> p t c", t=2) for L in LAYERS]
        n0_ps = [ps[:, u * 2048:(u + 1) * 2048].rearrange("p (t c) -> p t c", t=T) for u in range(2)]
        n1T_ps = [ps[:, u * 1024:(u + 1) * 1024].rearrange("p (k t n) -> p k t n", k=2, t=T) for u in range(2)]
        n1_ps = [[bank(4 + 2 * u + h, 2 * D).rearrange("p (t c) -> p t c", t=2) for h in range(2)] for u in range(2)]

        s_w = sem("weights_loaded")
        s_all = sem("edge_arrays_loaded")
        s_fill = sem("weights_cleared")
        s_scaled = sem("weights_scaled")
        s_const = sem("constants_made")
        s_pconst = sem("pool_constants_made")
        s_step = sem("constants_step")
        s_zero = [sem(f"table{l}_zeroed") for l in range(2)]
        s_src = sem2("src_loaded")
        s_attr = sem2("attr_loaded")
        s_drow = sem2("dst_row_loaded")
        s_gather = sem2("rows_gathered")
        s_scat = sem2("sums_scattered")
        s_ptick = sem("pool_waited")
        s_sptick = sem("sp_waited")
        s_xgT = sem("xg_turned")
        s_xgTsb = sem("xg_turned_copied")
        s_hid = sem("hidden_done")
        s_hidsb = sem("hidden_copied")
        s_h = sem("h_done")
        s_hs = sem("h_copied")
        s_wd = sem("edge_weights_done")
        s_ea = sem("edge_attr_scaled")
        s_prod = sem("dot_products_ready")
        s_dot1 = sem("dot_first_sum")
        s_dot2 = sem("dot_second_sum")
        s_cross = sem("cross_difference")
        s_mid = sem("products_ready")
        s_midT = sem("products_turned")
        s_midTsb = sem("products_turned_copied")
        s_o = sem("second_map_done")
        s_ms = sem("message_scalars_ready")
        s_pe1 = sem("message_vector_part")
        s_mv = sem("message_vectors_ready")
        s_dstf = sem("dst_as_float")
        s_tsp = sem("spare_distance")
        s_same = sem("same_dst_ready")
        s_nb = sem("duplicates_counted")
        s_lt = sem("later_edges_marked")
        s_lt2 = sem("later_edges_summed")
        s_row = sem("table_rows_ready")
        s_sum = sem("pair_summed")
        s_sumsb = sem("pair_sums_copied")

        s_nx = sem2("node_inputs_loaded")
        s_nT = sem("nodes_turned")
        s_nTsb = sem("nodes_turned_copied")
        s_np = sem("self_connection_done")
        s_pre = sem("preactivation_ready")
        s_gate = sem("gates_ready")
        s_f = sem("gated_ready")
        s_res = sem("residual_ready")
        s_bn = sem("stats_ready")
        s_p1, s_p2, s_p3, s_p4 = [sem(f"variance_step{n}") for n in range(4)]
        s_rstd = sem("rstd_ready")
        s_shift = sem("shift_ready")
        s_y = sem("y_ready")
        s_store = sem2("y_stored")
        s_q1 = sem("count_step1")
        s_q2 = sem("count_step2")
        s_q3 = sem("count_step3")
        s_q4 = sem("count_step4")

        loads = []
        for l, (w1, w2, l1s, l1v, scs, scv) in enumerate([
                ("L0_gnn_fc_w1", "L0_gnn_fc_w2", "L0_gnn_lin1_ws", "L0_gnn_lin1_wv", "L0_gnn_sc_ws", "L0_gnn_sc_wv"),
                ("L1_gnn_Wfc1", "L1_gnn_Wfc2", "L1_gnn_Wl1_0", "L1_gnn_Wl1_1", "L1_gnn_Wsc0", "L1_gnn_Wsc1")]):
            R = LAYERS[l]["R"]
            for t in range(2):
                loads.append((fc1[l][t * R:(t + 1) * R, t * H:(t + 1) * H], A[w1]))
                loads.append((fc2[l][t * H:(t + 1) * H, :], A[w2]))
            loads.append((lin1_s[l][:, :], A[l1s]))
            loads.append((self_s[l][:, :], A[scs]))
            for c in range(3):
                q = slice(c * V, (c + 1) * V)
                loads.append((lin1_v[l][q, q], A[l1v]))
                loads.append((self_v[l][q, q], A[scv]))
        ws, wv = A["L0_gnn_lin2_ws"], A["L0_gnn_lin2_wv"]
        loads.append((mapA[0][0:96, 0:96], ws))
        for c in range(3):
            loads.append((mapC[c * V:(c + 1) * V, c * V:(c + 1) * V], wv[96:128, :]))
        ws, wv1 = A["L1_gnn_Wl2_s"], A["L1_gnn_Wl2_v"]
        loads.append((mapA[1][0:96, 0:1], A["L1_gnn_Wa"]))
        loads.append((mapA[1][0:96, 1:65], ws))
        for l, w in ((0, wv), (1, wv1)):
            SO = LAYERS[l]["SO"]
            loads.append((mapA[l][96:128, SO:SO + V], w[64:96, :]))
            loads.append((mapB[l][0:32, 0:32], w[64:96, :]))
            loads.append((mapB[l][32:64, 32:64], w[64:96, :]))
            loads.append((mapB[l][64:128, 64:96], w[0:64, :]))

        i96 = 1 / math.sqrt(96.0)
        scales = [
            (fc1[0][:, :], 1 / 8), (fc1[1][:, :], 1 / 4),
            (fc2[0][:, 0:160], 1 / 8), (fc2[0][:, 160:192], 1 / 8 / math.sqrt(3.0)),
            (fc2[0][:, 192:224], 1 / 8 / math.sqrt(2.0)),
            (fc2[1][:, 0:160], 1 / 8), (fc2[1][:, 160:192], 1 / 8 / math.sqrt(3.0)),
            (mapA[0][:, 0:96], i96 / 4), (mapA[0][:, 96:128], 1 / math.sqrt(128.0) / 4),
            (mapB[0][:, :], 1 / math.sqrt(128.0) / 4), (mapC[:, :], 1 / math.sqrt(128.0) / 4),
            (mapA[1][:, :], i96), (mapB[1][:, :], i96)]
        for l in range(2):
            scales += [(lin1_s[l][:, :], 1 / 8), (self_s[l][:, :], 1 / 8),
                       (lin1_v[l][:, :], 1 / math.sqrt(32.0)), (self_v[l][:, :], 1 / math.sqrt(32.0))]
        cleared = [fc1[0], fc1[1], lin1_v[0], lin1_v[1], self_v[0], self_v[1],
                   mapA[0], mapA[1], mapB[0], mapB[1], mapC]

        block = ctx.enter_context(nc.Block())

        @block.sync
        def _(sp):
            sp.dma_start(dst_all[:, :], A["dst_col"]).then_inc(s_all, 16)
            sp.dma_start(attr_all[:, :, :].rearrange("p a b -> p (a b)"), A["attr6"]).then_inc(s_all, 16)
            sp.wait_ge(s_fill, 1)
            for dst, src in loads:
                sp.dma_start(dst, src).then_inc(s_w, 16)

            def clear_table(l):
                W = LAYERS[l]["ROW"]
                with sp.Fori(0, 24) as i:
                    sp.dma_start(table[l][bass.ds(i * 2048, 2048), :].rearrange("(p r) c -> p (r c)", p=P),
                                 zeros[:, 0:16 * W]).then_inc(s_zero[l], 16)
                r = (ROWS - 24 * 2048) // P
                sp.dma_start(table[l][24 * 2048:ROWS, :].rearrange("(p r) c -> p (r c)", p=P),
                             zeros[:, 0:r * W]).then_inc(s_zero[l], 16)

            clear_table(0)
            for l in range(2):
                base = l * NP

                def load_src(j, m, u):
                    wait_count(sp, s_gather[u], (j - 2 - u) * 16 + 32)
                    sp.dma_start(src_i[u][:, :], A["src_col"][bass.ds(m, 1)].rearrange("a p t -> p (a t)")).then_inc(s_src[u], 16)

                def load_attr(j, m, u):
                    wait_count(sp, s_hid, j - 1)
                    R2 = 2 * LAYERS[l]["R"]
                    sp.dma_start(attrT[u][0:R2, :], A[f"attrT{l}"][bass.ds(m, 1)].rearrange("a k e -> k (a e)")).then_inc(s_attr[u], 16)

                def load_dst_row(j, m, u):
                    wait_count(sp, s_same, j - 1)
                    sp.dma_start(dst_row[u][:, :], A["dst_row"][bass.ds(m, 1), :].partition_broadcast(P)).then_inc(s_drow[u], 16)

                run_stages(sp, base, NP, 4, [(0, load_src), (0, load_attr), (2, load_dst_row)])
                if l == 0:
                    clear_table(1)

                for u in range(2):
                    sp.wait_ge(s_scat[u], (l + 1) * NP * 16)

                def load_nodes(g, m, u):
                    wait_count(sp, s_res, g - 1)
                    sp.sem_inc(s_sptick, 1)
                    W = LAYERS[l]["ROW"]
                    if l == 0:
                        sp.dma_start(xsT[u][:, :], A["xsT"][bass.ds(m, 1)].rearrange("a k n -> k (a n)")).then_inc(s_nx[u], 16)
                        sp.dma_start(xvT[u][:, :], A["xvT"][bass.ds(m, 1)].rearrange("a k n -> k (a n)")).then_inc(s_nx[u], 16)
                    else:
                        sp.dma_start(x1g[u][:, :, :].rearrange("p t c -> p (t c)"),
                                     x1_rows[bass.ds(m * GROUP, GROUP), :].rearrange("(p t) c -> p (t c)", t=T)).then_inc(s_nx[u], 32)
                    sp.dma_start(tab[u][:, :, :].rearrange("p t c -> p (t c)")[:, 0:T * W],
                                 table[l][bass.ds(m * GROUP, GROUP), :].rearrange("(p t) c -> p (t c)", t=T)).then_inc(s_nx[u], 16)
                    sp.dma_start(a_n[u][:, :], A["a_node"][bass.ds(m, 1)].rearrange("a p t -> p (a t)")).then_inc(s_nx[u], 16)

                def store(g, m, u):
                    sp.wait_ge(s_y, g + 1)
                    to = x1_rows if l == 0 else out
                    sp.dma_start(to[bass.ds(m * GROUP, GROUP), :].rearrange("(p t) c -> p (t c)", t=T),
                                 y[u][:, :, :].rearrange("p t c -> p (t c)")).then_inc(s_store[u], 16)

                if l == 1:
                    pass
                run_stages(sp, l * NG, NG, 4, [(0, load_nodes), (3, store)])
                for u in range(2):
                    sp.wait_ge(s_store[u], (l + 1) * NG * 8)

        @block.gpsimd
        def _(pool):
            nc.gpsimd.memset(ident[:, :], 0.0)
            nc.gpsimd.memset(earlier[:, :], 1.0)
            nc.gpsimd.memset(minus_half[:, :], -0.5)
            nc.gpsimd.memset(quarter[:, :], 0.25)
            nc.gpsimd.iota(spare_i[:, :], pattern=[[P, 2]], base=N_PAD, channel_multiplier=1).then_inc(s_step, 1)
            pool.wait_ge(s_step, 1)
            nc.gpsimd.affine_select(out=ident[:, :], in_=ident[:, :], compare_op=ALU.not_equal, fill=1.0,
                                    base=0, pattern=[[-1, P]], channel_multiplier=1)
            nc.gpsimd.affine_select(out=earlier[:, :], in_=earlier[:, :], compare_op=ALU.is_gt, fill=0.0,
                                    base=0, pattern=[[-1, P]], channel_multiplier=1)
            nc.gpsimd.tensor_copy(spare_row[:, :], spare_i[:, :]).then_inc(s_pconst, 1)
            for l in range(2):
                rows, width = (A["x_rows"], D + 1) if l == 0 else (x1_rows, D)

                def gather(j, m, u):
                    wait_count(pool, s_xgT, j - 1)
                    wait_count(pool, s_ea, j - 1)
                    pool.wait_ge(s_src[u], (j - u) * 8 + 16)
                    pool.sem_inc(s_ptick, 1)
                    for t in range(2):
                        pool.indirect_dma_start(
                            out=xg[u][:, t, 0:width], out_offset=None, in_=rows,
                            in_offset=bass.IndirectOffsetOnAxis(ap=src_i[u][:, t:t + 1], axis=0)).then_inc(s_gather[u], 16)

                def scatter(j, m, u):
                    wait_count(pool, s_sumsb, j + 1)
                    wait_count(pool, s_row, j + 1)
                    wait_count(pool, s_scat[1 - u], (j - 1 - (1 - u)) * 16 + 32)
                    pool.sem_inc(s_ptick, 1)
                    W = LAYERS[l]["ROW"]
                    for t in range(2):
                        pool.indirect_dma_start(
                            out=table[l], out_offset=bass.IndirectOffsetOnAxis(ap=row_i[u][:, t:t + 1], axis=0),
                            in_=sums[u][:, t, 0:W], in_offset=None, compute_op=ALU.add).then_inc(s_scat[u], 16)

                if l == 1:
                    for u in range(2):
                        pool.wait_ge(s_store[u], NG * 8)
                pool.wait_ge(s_zero[l], 25 * 16)
                run_stages(pool, l * NP, NP, 8, [(0, gather), (6, scatter)])

                def powers(g, m, u):
                    st = stats[u]
                    tt, ts = nc.gpsimd.tensor_tensor, nc.gpsimd.tensor_scalar
                    pool.wait_ge(s_bn, g + 1)
                    wait_count(pool, s_y, g - 1)
                    tt(mean2[:, :], st[:, :, 1], st[:, :, 4], ALU.add)
                    tt(apart[:, :], st[:, :, 1], st[:, :, 4], ALU.subtract)
                    tt(squares[:, :], st[:, :, 2], st[:, :, 5], ALU.add).then_inc(s_p1, 1)
                    pool.wait_ge(s_p1, g + 1)
                    tt(apart2[:, :], apart[:, :], apart[:, :], ALU.mult)
                    ts(neg_mean[:, :], mean2[:, :], -0.5, None, ALU.mult)
                    ts(var_in[:, :], squares[:, :], 1.0 / D, EPS, ALU.mult, ALU.add).then_inc(s_p2, 1)
                    pool.wait_ge(s_p2, g + 1)
                    tt(apart2[:, :], apart2[:, :], quarter[:, :], ALU.mult).then_inc(s_p3, 1)
                    pool.wait_ge(s_p3, g + 1)
                    tt(var_e[:, :], var_in[:, :], apart2[:, :], ALU.add).then_inc(s_p4, 1)
                    pool.wait_ge(s_p4, g + 1)
                    tt(rstd[u][:, :], var_e[:, :], minus_half[:, :], ALU.pow).then_inc(s_rstd, 1)
                    pool.wait_ge(s_rstd, g + 1)
                    tt(shift[u][:, :], neg_mean[:, :], rstd[u][:, :], ALU.mult).then_inc(s_shift, 1)

                run_stages(pool, l * NG, NG, 2, [(0, powers)])

        @block.tensor
        def _(pe):
            mm, turn = nc.tensor.matmul, nc.tensor.transpose
            pe.wait_ge(s_scaled, 1)
            pe.wait_ge(s_pconst, 1)
            for l in range(2):
                L = LAYERS[l]
                SO, R2 = L["SO"], 2 * L["R"]

                def turn_x(j, m, u):
                    pe.wait_ge(s_gather[u], (j - u) * 16 + 32)
                    wait_count(pe, s_xgTsb, j)
                    for t in range(2):
                        turn(xgT_ps[0:96, 2 + t, :], xg[u][:, t, S:D], ident[:, :])
                        last = turn(xgT_ps[0:S, t, :], xg[u][:, t, 0:S], ident[:, :])
                    last.then_inc(s_xgT, 1)

                def hidden(j, m, u):
                    pe.wait_ge(s_attr[u], (j - u) * 8 + 16)
                    wait_count(pe, s_hidsb, j)
                    mm(hidT_ps, fc1[l][0:R2, :], attrT[u][0:R2, :], start=True, stop=True).then_inc(s_hid, 1)

                def first_map(j, m, u):
                    pe.wait_ge(s_xgTsb, j + 1)
                    wait_count(pe, s_hs, j)
                    pe.wait_ge(s_hidsb, j + 1)
                    for t in range(2):
                        mm(h_ps[:, t, 0:S], xgT[u][0:S, t, :], lin1_s[l][:, :], start=True, stop=True)
                        last = mm(h_ps[:, t, S:D], xgT[u][0:96, 2 + t, :], lin1_v[l][:, :], start=True, stop=True)
                    last.then_inc(s_h, 1)

                def edge_weights(j, m, u):
                    wait_count(pe, s_mid, j)
                    for t in range(2):
                        q = slice(t * H, (t + 1) * H)
                        last = mm(w_ps[l][:, t, :], hidT[u][q, :], fc2[l][q, :], start=True, stop=True)
                    last.then_inc(s_wd, 1)

                def turn_mid(j, m, u):
                    pe.wait_ge(s_mid, j + 1)
                    wait_count(pe, s_midTsb, j)
                    for c in range(2):
                        for t in range(2):
                            last = turn(midT_ps[:, 2 * c + t, :], mid[u][:, t, c * P:(c + 1) * P], ident[:, :])
                    if L["cross"]:
                        for t in range(2):
                            last = turn(midT_ps[0:96, 4 + t, :], mid[u][:, t, 256:352], ident[:, :])
                    last.then_inc(s_midT, 1)

                def second_map(j, m, u):
                    pe.wait_ge(s_midTsb, j + 1)
                    wait_count(pe, s_ms, j)
                    wait_count(pe, s_mv, j)
                    for t in range(2):
                        mm(o_ps[l][:, t, 0:SO + V], midT[u][:, t, :], mapA[l][:, :], start=t == 0, stop=not L["cross"],
                           skip_group_check=True)
                        last = mm(o_ps[l][:, t, SO + V:SO + 4 * V], midT[u][:, 2 + t, :], mapB[l][:, :], start=False,
                                  stop=not L["cross"], skip_group_check=True)
                        if L["cross"]:
                            last = mm(o_ps[l][:, t, SO:SO + 3 * V], midT[u][0:96, 4 + t, :], mapC[:, :], start=False,
                                      stop=True, skip_group_check=True)
                    last.then_inc(s_o, 1)

                def sum_pair(j, m, u):
                    pe.wait_ge(s_ms, j + 1)
                    pe.wait_ge(s_mv, j + 1)
                    pe.wait_ge(s_same, j + 1)
                    wait_count(pe, s_sumsb, j)
                    mm(sum_ps[l][:, 0, :], same0[u][:, :], msg[l][u][:, 0, :], start=True, stop=False)
                    mm(sum_ps[l][:, 0, :], same1[u][:, 0:P], msg[l][u][:, 1, :], start=False, stop=True)
                    mm(sum_ps[l][:, 1, :], same1[u][:, P:PAIR], msg[l][u][:, 1, :], start=True, stop=True).then_inc(s_sum, 1)

                if l == 1:
                    pe.wait_ge(s_res, NG)
                run_stages(pe, l * NP, NP, 6, [(1, first_map), (0, hidden), (1, edge_weights), (0, turn_x),
                                               (3, second_map), (2, turn_mid), (4, sum_pair)])

                def nodes0(g, m, u):
                    pe.wait_ge(s_nx[u], (g - u) * 32 + 64)
                    wait_count(pe, s_res, g - 1)
                    for t in range(T):
                        q = slice(t * P, (t + 1) * P)
                        mm(n0_ps[u][:, t, 0:96], xsT[u][:, q], self_s[0][:, :], start=True, stop=True)
                        mm(n0_ps[u][:, t, 96:192], xvT[u][:, q], self_v[0][:, :], start=True, stop=True)
                        turn(n0_ps[u][:, t, 192:256], xsT[u][:, q], ident[0:S, 0:S])
                        last = turn(n0_ps[u][:, t, 256:352], xvT[u][:, q], ident[0:96, 0:96])
                    last.then_inc(s_np, 1)

                def turn1(g, m, u):
                    pe.wait_ge(s_nx[u], (g - u) * 32 + 64)
                    wait_count(pe, s_nTsb, g - 1 - NG)
                    for t in range(T):
                        turn(n1T_ps[u][0:96, 1, t, :], x1g[u][:, t, S:D], ident[:, :])
                        last = turn(n1T_ps[u][0:S, 0, t, :], x1g[u][:, t, 0:S], ident[:, :])
                    last.then_inc(s_nT, 1)

                def nodes1(g, m, u):
                    pe.wait_ge(s_nTsb, g + 1 - NG)
                    wait_count(pe, s_res, g - 1)
                    for t in range(T):
                        q = slice(t * P, (t + 1) * P)
                        o = n1_ps[u][t // 2]
                        mm(o[:, t % 2, 0:S], xsT[u][:, q], self_s[1][:, :], start=True, stop=True)
                        last = mm(o[:, t % 2, S:D], xvT[u][:, q], self_v[1][:, :], start=True, stop=True)
                    last.then_inc(s_np, 1)

                pe.wait_ge(s_sumsb, (l + 1) * NP)
                if l == 0:
                    run_stages(pe, 0, NG, 2, [(0, nodes0)])
                else:
                    run_stages(pe, NG, NG, 4, [(0, turn1), (1, nodes1)])

        @block.scalar
        def _(act):
            copy = nc.scalar.copy
            for l in range(2):
                L = LAYERS[l]
                SO, W = L["SO"], L["ROW"]

                def copy_h(j, m, u):
                    act.wait_ge(s_h, j + 1)
                    if not (isinstance(j, int) and j == (l + 1) * NP - 1):
                        act.wait_ge(s_hid, j + 2)
                    wait_count(act, s_mid, j - 1)
                    copy(hs[u][:, :, 0:D], h_ps[:, :, :])
                    copy(hs[u][:, :, D:D + 2 * V], h_ps[:, :, S:S + 2 * V]).then_inc(s_hs, 1)

                def hidden_act(j, m, u):
                    act.wait_ge(s_hid, j + 1)
                    wait_count(act, s_wd, j - 1)
                    nc.scalar.activation(hidT[u][:, :], hidT_ps, ACT.Silu).then_inc(s_hidsb, 1)

                def copy_xT(j, m, u):
                    act.wait_ge(s_xgT, j + 1)
                    wait_count(act, s_h, j - 1)
                    copy(xgT[u][0:S, 0:2, :], xgT_ps[0:S, 0:2, :])
                    copy(xgT[u][0:96, 2:4, :], xgT_ps[0:96, 2:4, :]).then_inc(s_xgTsb, 1)

                def copy_message(j, m, u):
                    act.wait_ge(s_o, j + 1)
                    wait_count(act, s_sum, j - 1)
                    copy(msg[l][u][:, :, 0:SO], o_ps[l][:, :, 0:SO]).then_inc(s_ms, 1)

                def copy_midT(j, m, u):
                    act.wait_ge(s_midT, j + 1)
                    wait_count(act, s_o, j - 1)
                    last = copy(midT[u][:, 0:4, :], midT_ps[:, 0:4, :])
                    if L["cross"]:
                        last = copy(midT[u][0:96, 4:6, :], midT_ps[0:96, 4:6, :])
                    last.then_inc(s_midTsb, 1)

                def copy_sums(j, m, u):
                    act.wait_ge(s_sum, j + 1)
                    wait_count(act, s_scat[u], (j - 2 - u) * 16 + 32)
                    copy(sums[u][:, :, 0:W], sum_ps[l][:, :, :]).then_inc(s_sumsb, 1)

                run_stages(act, l * NP, NP, 6, [(1, copy_h), (0, copy_xT), (0, hidden_act),
                                                (3, copy_message), (2, copy_midT), (4, copy_sums)])

                def gates(g, m, u):
                    act.wait_ge(s_pre, g + 1)
                    wait_count(act, s_f, g - 1)
                    for t in range(T):
                        last = nc.scalar.activation(gate[u][:, t, :], pre[u][:, t, 0:96], ACT.Sigmoid,
                                                    scale=a_n[u][:, t:t + 1])
                    last.then_inc(s_gate, 1)

                def copy_nT(g, m, u):
                    act.wait_ge(s_nT, g + 1 - NG)
                    wait_count(act, s_np, g - 1)
                    copy(xsT[u][:, :].rearrange("p (t n) -> p t n", t=T), n1T_ps[u][0:S, 0, :, :])
                    copy(xvT[u][:, :].rearrange("p (t n) -> p t n", t=T), n1T_ps[u][0:96, 1, :, :]).then_inc(s_nTsb, 1)

                def normalise(g, m, u):
                    act.wait_ge(s_shift, g + 1)
                    wait_count(act, s_store[u], (g - 2 - u) * 8 + 16)
                    for t in range(T):
                        last = nc.scalar.activation(y[u][:, t, :], res[u][:, t, :], ACT.Identity,
                                                    scale=rstd[u][:, t:t + 1], bias=shift[u][:, t:t + 1])
                    last.then_inc(s_y, 1)

                run_stages(act, l * NG, NG, 4, [(0, gates if l == 0 else copy_nT), (2, normalise)])

        @block.vector
        def _(dve):
            tt, stt = nc.vector.tensor_tensor, nc.vector.scalar_tensor_tensor
            for w in cleared:
                nc.vector.memset(w[:, :], 0.0)
            for u in range(2):
                nc.vector.memset(msg[1][u][:, :, 161:162], 1.0)
            nc.vector.memset(zeros[:, :], 0.0).then_inc(s_fill, 1)
            dve.wait_ge(s_w, 16 * len(loads))
            dve.wait_ge(s_fill, 1)
            for w, f in scales:
                last = nc.vector.tensor_scalar(w, w, f, None, ALU.mult)
            last.then_inc(s_scaled, 1)
            dve.wait_ge(s_all, 32)
            dve.wait_ge(s_pconst, 1)

            def planes(ap):
                return ap.rearrange("p t (i c) -> p t i c", c=V)

            for l in range(2):
                L = LAYERS[l]
                SO = L["SO"]

                def scale_attr(j, m, u):
                    wait_count(dve, s_mid, j - 1)
                    at = bass.ds(m * 2, 2)
                    if l == 0:
                        dve.wait_ge(s_gather[u], (j - u) * 16 + 32)
                        a = xg[u][:, :, D:D + 1].to_broadcast([P, 2, 6])
                        tt(ea[u][:, :, :], attr_all[:, at, :], a, ALU.mult)
                        tt(ea_all[:, at, :], attr_all[:, at, :], a, ALU.mult).then_inc(s_ea, 1)
                    else:
                        nc.vector.tensor_copy(ea[u][:, :, :], ea_all[:, at, :]).then_inc(s_ea, 1)

                def products(j, m, u):
                    dve.wait_ge(s_hs, j + 1)
                    dve.wait_ge(s_ea, j + 1)
                    wait_count(dve, s_midT, j - 1)
                    h, e, w, o = hs[u], ea[u], w_ps[l], mid[u]
                    hv = h[:, :, S:D + 2 * V].rearrange("p t (i c) -> p t i c", c=V)

                    def comp(k):
                        return e[:, :, k:k + 3].unsqueeze(3).to_broadcast([P, 2, 3, V])

                    tt(planes(prod[:, :, :]), hv[:, :, 0:3, :], comp(1), ALU.mult).then_inc(s_prod, 1)
                    if L["cross"]:
                        tt(planes(crossA[:, :, :]), hv[:, :, 1:4, :], comp(3), ALU.mult)
                        tt(planes(crossB[:, :, :]), hv[:, :, 2:5, :], comp(2), ALU.mult)
                    dve.wait_ge(s_prod, j + 1)
                    last = tt(dot[:, :, :], prod[:, :, 0:V], prod[:, :, V:2 * V], ALU.add)
                    last.then_inc(s_dot1, 1)
                    dve.wait_ge(s_wd, j + 1)
                    tt(o[:, :, 192:256], h[:, :, 0:S], w[:, :, 64:128], ALU.mult)
                    for t in range(2):
                        stt(o[:, t, 0:S], h[:, t, 0:S], e[:, t, 0:1], w[:, t, 0:S], ALU.mult, ALU.mult)
                    dve.wait_ge(s_dot1, j + 1)
                    tt(dot[:, :, :], dot[:, :, :], prod[:, :, 2 * V:3 * V], ALU.add).then_inc(s_dot2, 1)
                    if L["cross"]:
                        tt(crossA[:, :, :], crossA[:, :, :], crossB[:, :, :], ALU.subtract).then_inc(s_cross, 1)
                    for t in range(2):
                        stt(o[:, t, 96:192].rearrange("p (i c) -> p i c", c=V), hv[:, t, 0:3, :], e[:, t, 0:1],
                            w[:, t:t + 1, 128:160].to_broadcast([P, 3, V]), ALU.mult, ALU.mult)
                    dve.wait_ge(s_dot2, j + 1)
                    last = tt(o[:, :, S:S + V], dot[:, :, :], w[:, :, 160:192], ALU.mult)
                    if L["cross"]:
                        dve.wait_ge(s_cross, j + 1)
                        last = tt(planes(o[:, :, 256:352]), planes(crossA[:, :, :]),
                                  w[:, :, 192:224].unsqueeze(2).to_broadcast([P, 2, 3, V]), ALU.mult)
                    last.then_inc(s_mid, 1)

                def message_vectors(j, m, u):
                    dve.wait_ge(s_ms, j + 1)
                    wait_count(dve, s_sum, j - 1)
                    e1 = ea_all[:, bass.ds(m * 2, 2), 1:4].unsqueeze(3).to_broadcast([P, 2, 3, V])
                    p32 = o_ps[l][:, :, SO + 3 * V:SO + 4 * V].unsqueeze(2).to_broadcast([P, 2, 3, V])
                    tt(planes(pe1[u][:, :, :]), p32, e1, ALU.mult).then_inc(s_pe1, 1)

                def message_sum(j, m, u):
                    dve.wait_ge(s_pe1, j + 1)
                    tt(msg[l][u][:, :, SO:SO + 3 * V], pe1[u][:, :, :], o_ps[l][:, :, SO:SO + 3 * V], ALU.add).then_inc(s_mv, 1)

                def compare(j, m, u):
                    at = bass.ds(m * 2, 2)
                    wait_count(dve, s_same, j)
                    if l == 0:
                        wait_count(dve, s_row, j)
                    nc.vector.tensor_copy(dst_f[:, :], dst_all[:, at]).then_inc(s_dstf, 1)
                    dve.wait_ge(s_drow[u], (j - u) * 8 + 16)
                    wait_count(dve, s_sum, j - 1)
                    dve.wait_ge(s_dstf, j + 1)
                    nc.vector.tensor_scalar(same0[u][:, :], dst_row[u][:, 0:P], dst_f[:, 0:1], None, ALU.is_equal)
                    nc.vector.tensor_scalar(same1[u][:, :], dst_row[u][:, :], dst_f[:, 1:2], None, ALU.is_equal).then_inc(s_same, 1)
                    wait_count(dve, s_scat[u], (j - 2 - u) * 16 + 32)
                    if l == 1:
                        nc.vector.tensor_copy(row_i[u][:, :], row_all[:, at]).then_inc(s_row, 1)

                def choose_rows(j, m, u):
                    at = bass.ds(m * 2, 2)
                    tt(to_spare[:, :], spare_row[:, :], dst_f[:, :], ALU.subtract)
                    dve.wait_ge(s_same, j + 1)
                    ttr = nc.vector.tensor_tensor_reduce
                    ttr(out=junk[:, 0:P], in0=same0[u][:, :], in1=earlier[:, :], scale=1.0, scalar=0.0,
                        op0=ALU.mult, op1=ALU.add, accum_out=n_before[:, 0:1])
                    ttr(out=junk[:, P:PAIR], in0=same1[u][:, P:PAIR], in1=earlier[:, :], scale=1.0, scalar=0.0,
                        op0=ALU.mult, op1=ALU.add, accum_out=n_before[:, 1:2])
                    nc.vector.tensor_reduce(n_before[:, 2:3], same1[u][:, 0:P], mybir.AxisListType.X, ALU.add).then_inc(s_nb, 1)
                    dve.wait_ge(s_nb, j + 1)
                    tt(n_before[:, 1:2], n_before[:, 1:2], n_before[:, 2:3], ALU.add).then_inc(s_lt2, 1)
                    dve.wait_ge(s_lt2, j + 1)
                    stt(later[:, :], n_before[:, 0:2], 1.0, to_spare[:, :], ALU.min, ALU.mult).then_inc(s_lt, 1)
                    dve.wait_ge(s_lt, j + 1)
                    tt(row_i[u][:, :], later[:, :], dst_f[:, :], ALU.add)
                    tt(row_all[:, at], later[:, :], dst_f[:, :], ALU.add).then_inc(s_row, 1)

                run_stages(dve, l * NP, NP, 6, [(3, message_vectors), (0, scale_attr), (3, message_sum), (3, compare)]
                           + [(3, choose_rows)] * (l == 0) + [(1, products)])

                def gated0(g, m, u):
                    dve.wait_ge(s_gate, g + 1)
                    wait_count(dve, s_y, g - 1)
                    for t in range(T):
                        a = a_n[u][:, t:t + 1]
                        stt(res[u][:, t, 0:S], pre[u][:, t, 0:S], a, gate[u][:, t, 0:S], ALU.mult, ALU.mult)
                        last = stt(res[u][:, t, S:D].rearrange("p (i c) -> p i c", c=V),
                                   pre[u][:, t, 96:192].rearrange("p (i c) -> p i c", c=V), a,
                                   gate[u][:, t:t + 1, S:96].to_broadcast([P, 3, V]), ALU.mult, ALU.mult)
                    last.then_inc(s_f, 1)

                def pre0(g, m, u):
                    dve.wait_ge(s_np, g + 1)
                    wait_count(dve, s_f, g - 1)
                    tt(pre[u][:, :, :], n0_ps[u][:, :, 0:192], tab[u][:, :, :], ALU.add).then_inc(s_pre, 1)

                def residual0(g, m, u):
                    dve.wait_ge(s_f, g + 1)
                    tt(res[u][:, :, :], res[u][:, :, :], n0_ps[u][:, :, 192:352], ALU.add).then_inc(s_res, 1)

                def residual1(g, m, u):
                    W = LAYERS[1]["ROW"]
                    tb = tab[u][:, :, :].rearrange("p t c -> p (t c)")[:, 0:T * W].rearrange("p (t c) -> p t c", c=W)
                    q = small[u]
                    dve.wait_ge(s_nx[u], (g - u) * 32 + 64)
                    nc.vector.tensor_scalar(q[:, :, 0], tb[:, :, 161], 1.0, None, ALU.max).then_inc(s_q1, 1)
                    dve.wait_ge(s_np, g + 1)
                    wait_count(dve, s_y, g - 1)
                    for t in range(2):
                        stt(res[u][:, t, :], n1_ps[u][0][:, t, :], a_n[u][:, t:t + 1], x1g[u][:, t, :], ALU.mult, ALU.add)
                    dve.wait_ge(s_q1, g + 1 - NG)
                    nc.vector.reciprocal(q[:, :, 1], q[:, :, 0]).then_inc(s_q2, 1)
                    stt(res[u][:, 2, :], n1_ps[u][1][:, 0, :], a_n[u][:, 2:3], x1g[u][:, 2, :], ALU.mult, ALU.add)
                    dve.wait_ge(s_q2, g + 1 - NG)
                    tt(q[:, :, 2], q[:, :, 1], a_n[u][:, :], ALU.mult).then_inc(s_q3, 1)
                    stt(res[u][:, 3, :], n1_ps[u][1][:, 1, :], a_n[u][:, 3:4], x1g[u][:, 3, :], ALU.mult, ALU.add)
                    dve.wait_ge(s_q3, g + 1 - NG)
                    tt(q[:, :, 3], q[:, :, 2], q[:, :, 2], ALU.mult).then_inc(s_q4, 1)
                    dve.wait_ge(s_q4, g + 1 - NG)
                    tt(q[:, :, 0], q[:, :, 3], tb[:, :, 0], ALU.mult).then_inc(s_f, 1)
                    dve.wait_ge(s_f, g + 1)
                    for t in range(T):
                        last = stt(res[u][:, t, :], tb[:, t, 1:161], q[:, t, 0:1], res[u][:, t, :], ALU.mult, ALU.add)
                    last.then_inc(s_res, 1)

                def stats_of(g, m, u):
                    dve.wait_ge(s_res, g + 1)
                    wait_count(dve, s_shift, g - 1)
                    for t in range(T):
                        last = nc.vector.bn_stats(stats[u][:, t, :], res[u][:, t, :])
                    last.then_inc(s_bn, 1)

                if l == 0:
                    run_stages(dve, 0, NG, 4, [(0, pre0), (1, gated0), (1, residual0), (1, stats_of)])
                else:
                    run_stages(dve, NG, NG, 2, [(0, residual1), (0, stats_of)])


_WEIGHTS = [
    "L0_gnn_lin1_ws", "L0_gnn_lin1_wv", "L0_gnn_fc_w1", "L0_gnn_fc_w2", "L0_gnn_sc_ws", "L0_gnn_sc_wv",
    "L0_gnn_lin2_ws", "L0_gnn_lin2_wv", "L1_gnn_Wfc1", "L1_gnn_Wfc2", "L1_gnn_Wsc0", "L1_gnn_Wsc1",
    "L1_gnn_Wl1_0", "L1_gnn_Wl1_1", "L1_gnn_Wl2_s", "L1_gnn_Wl2_v", "L1_gnn_Wa"]


def kernel(**inputs):
    import concourse.bacc as bacc
    from concourse.bass_utils import run_bass_kernel_spmd

    g = {k: np.asarray(v) for k, v in inputs.items()}
    x, a = g["x"], g["node_vec1"]
    planar = np.concatenate([x[:, :S], x[:, S:].reshape(N, V, 3).transpose(0, 2, 1).reshape(N, 3 * V)], 1)
    padded = np.zeros((N_PAD, D), x.dtype)
    padded[:N] = planar
    turned = padded.reshape(NG, P, T, D).transpose(0, 3, 2, 1).reshape(NG, D, GROUP)
    a_node = np.zeros(N_PAD, a.dtype)
    a_node[:N] = a[:, 0]

    def edges(v, fill=0):
        p = np.full((NP * PAIR,) + v.shape[1:], fill, v.dtype)
        p[:E] = v
        return p.reshape((NP, 2, P) + v.shape[1:])

    src, dst = edges(g["src"]), edges(g["dst"], N)
    attr = edges(g["edge_attr_4"])[..., [0, 1, 2, 3, 1, 2]]
    arrays = {
        "x_rows": np.concatenate([planar, a], 1),
        "xsT": turned[:, :S], "xvT": turned[:, S:],
        "a_node": a_node.reshape(NG, P, T),
        "src_col": src.transpose(0, 2, 1),
        "dst_col": dst.transpose(2, 0, 1).reshape(P, NP * 2),
        "dst_row": dst.reshape(NP, PAIR),
        "attr6": attr.transpose(2, 0, 1, 3).reshape(P, NP * 12),
        "attrT0": edges(g["edge_attr_64"]).transpose(0, 1, 3, 2).reshape(NP, 128, P),
        "attrT1": edges(g["edge_attr_16"]).transpose(0, 1, 3, 2).reshape(NP, 32, P),
        **{k: g[k] for k in _WEIGHTS},
    }
    arrays = {f"in_{k}": np.ascontiguousarray(v) for k, v in arrays.items()}
    nc = bacc.Bacc("TRN2", target_bir_lowering=False, num_devices=1)
    aps = {k[3:]: nc.dram_tensor(k, v.shape, mybir.dt.from_np(v.dtype), kind="ExternalInput").ap()
           for k, v in arrays.items()}
    out = nc.dram_tensor("out_rows", (N_PAD, D), F32, kind="ExternalOutput").ap()
    program(nc, aps, out)
    r = run_bass_kernel_spmd(nc, [arrays], core_ids=[0]).results[0]["out_rows"]
    r = np.asarray(r)[:N]
    return np.concatenate([r[:, :S], r[:, S:].reshape(N, 3, V).transpose(0, 2, 1).reshape(N, 3 * V)], 1)
```

```python
import math

import numpy as np
import concourse.bass as bass
from concourse import mybir
from contextlib import ExitStack

F32 = mybir.dt.float32
I32 = mybir.dt.int32
ALU = mybir.AluOpType
ACT = mybir.ActivationFunctionType

P = 128
N, E = 50000, 25000
S, V = 64, 32
D = S + 3 * V
PAIR = 2 * P
NP = -(-E // PAIR)
T = 4
GROUP = T * P
NG = -(-N // GROUP)
N_PAD = NG * GROUP
ROWS = N_PAD + PAIR
H = 64
EPS = 1e-5

LAYERS = [
    dict(R=64, W=224, SO=96, SG=96, ROW=192, cross=True),
    dict(R=16, W=192, SO=65, SG=64, ROW=162, cross=False),
]


def wait_count(eng, sem, n):
    if not isinstance(n, int) or n > 0:
        eng.wait_ge(sem, n)


def run_stages(eng, base, count, depth, stages):
    assert (count - depth) % 4 == 0
    for k in range(base, base + depth):
        for lag, f in stages:
            if k - lag >= base:
                f(k - lag, k - lag - base, (k - lag) % 4)
    with eng.Fori(base + depth, base + count - 3, 4) as i:
        for r in range(4):
            for lag, f in stages:
                f(i + (r - lag), i + (r - lag - base), (base + depth + r - lag) % 4)
    for k in range(base + count, base + count + depth):
        for lag, f in stages:
            if k - lag < base + count:
                f(k - lag, k - lag - base, (k - lag) % 4)


def landed(j, turn, ring, per=16):
    return (j - turn) * (per // ring) + per


def program(nc, A, out):
    ctx = ExitStack()
    with ctx:
        def sb(name, shape, dt=F32):
            return ctx.enter_context(nc.sbuf_tensor(name, shape, dt))

        def two(name, shape, dt=F32):
            return [sb(f"{name}{u}", shape, dt) for u in range(2)] * 2

        def four(name, shape, dt=F32):
            return [sb(f"{name}{u}", shape, dt) for u in range(4)]

        def sem(name):
            return ctx.enter_context(nc.semaphore(name))

        def sem2(name):
            return [sem(f"{name}{u}") for u in range(2)] * 2

        def sem4(name):
            return [sem(f"{name}{u}") for u in range(4)]

        def dram(name, shape):
            return nc.dram_tensor(name, shape, F32, kind="Internal").ap()

        x1_rows = dram("x1_rows", (N_PAD, D))
        table = [dram(f"table{l}", (ROWS, LAYERS[l]["ROW"])) for l in range(2)]

        ident = sb("ident", [P, P])
        fc1 = [sb("fc1_0", [P, 2 * H]), sb("fc1_1", [32, 2 * H])]
        fc2 = [sb(f"fc2_{l}", [P, LAYERS[l]["W"]]) for l in range(2)]
        lin1_s = [sb(f"lin1_s{l}", [S, S]) for l in range(2)]
        lin1_v = [sb(f"lin1_v{l}", [3 * V, 3 * V]) for l in range(2)]
        mapA = [sb(f"mapA{l}", [P, LAYERS[l]["SO"] + V]) for l in range(2)]
        mapB = [sb(f"mapB{l}", [P, 3 * V]) for l in range(2)]
        mapC = sb("mapC", [3 * V, 3 * V])
        self_s = [sb(f"self_s{l}", [S, LAYERS[l]["SG"]]) for l in range(2)]
        self_v = [sb(f"self_v{l}", [3 * V, 3 * V]) for l in range(2)]
        zeros = sb("zeros", [P, 16 * 192])
        earlier = sb("earlier", [P, PAIR])
        spare_row = sb("spare_row", [P, NP, 2])
        spare_i = sb("spare_i", [P, NP, 2], I32)
        minus_half = sb("minus_half", [P, T])
        quarter = sb("quarter", [P, T])

        dst_all = sb("dst_all", [P, NP * 2], I32)
        attr_all = sb("attr_all", [P, NP * 2, 6])
        ea_all = sb("ea_all", [P, NP * 2, 6])
        row_all = sb("row_all", [P, NP * 2], I32)
        dst_f = sb("dst_f", [P, NP * 2])
        to_spare = sb("to_spare", [P, NP * 2])
        a_all = sb("a_all", [P, NG, T])

        src_i = four("src_i", [P, 2], I32)
        xg = four("xg", [P, 2, D + 1])
        attrT = four("attrT", [P, P])
        dst_row = four("dst_row", [P, PAIR], I32)
        xgT = two("xgT", [P, 4, P])
        hidT = two("hidT", [P, P])
        hs = two("hs", [P, 2, D + 2 * V])
        mid = two("mid", [P, 2, 352])
        midT = two("midT", [P, 6, P])
        msg = [two(f"msg{l}_", [P, 2, LAYERS[l]["ROW"]]) for l in range(2)]
        pe1 = two("pe1", [P, 2, 3 * V])
        same0 = two("same0", [P, P])
        same1 = two("same1", [P, PAIR])
        sums = two("sums", [P, 2, 192])
        row_i = two("row_i", [P, 2], I32)
        prod = two("prod", [P, 2, 3 * V])
        crossA = two("crossA", [P, 2, 3 * V])
        crossB = two("crossB", [P, 2, 3 * V])
        dot = two("dot", [P, 2, V])
        is_later = two("is_later", [P, 2])
        step = two("step", [P, 2])
        junk = sb("junk", [P, 3 * P])

        xsT = four("xsT", [S, GROUP])
        xvT = four("xvT", [3 * V, GROUP])
        x1g = four("x1g", [P, T, D])
        tab = four("tab", [P, T, 192])
        pre = two("pre", [P, T, 192])
        gate = two("gate", [P, T, 96])
        res = four("res", [P, T, D])
        stats = two("stats", [P, T, 6])
        mean2, apart, squares, apart2, var_in, var_e, neg_mean = [
            sb(n, [P, T]) for n in ("mean2", "apart", "squares", "apart2", "var_in", "var_e", "neg_mean")]
        rstd = four("rstd", [P, T])
        shift = four("shift", [P, T])
        y = two("y", [P, T, D])
        small = two("small", [P, T, 4])

        ps = ctx.enter_context(nc.psum_tensor("ps", [P, 8 * 512], F32))

        def bank(b, n=512):
            return ps[:, b * 512:b * 512 + n]

        xgT_ps = bank(0).rearrange("p (k e) -> p k e", k=4)
        hidT_ps = bank(1)[:, 384:512]
        h_ps = bank(1, 2 * D).rearrange("p (t c) -> p t c", t=2)
        w_ps = [ps[:, 1024:2048].rearrange("p (t c) -> p t c", t=2)[:, :, 0:L["W"]] for L in LAYERS]
        midT_ps = bank(4, 768).rearrange("p (k e) -> p k e", k=6)
        o_ps = [bank(6, 2 * (L["SO"] + 128)).rearrange("p (t c) -> p t c", t=2) for L in LAYERS]
        sum_ps = [bank(7, 2 * L["ROW"]).rearrange("p (t c) -> p t c", t=2) for L in LAYERS]
        n0_ps = [ps[:, u * 2048:(u + 1) * 2048].rearrange("p (t c) -> p t c", t=T) for u in range(2)]
        n1T_ps = [ps[:, u * 1024:(u + 1) * 1024].rearrange("p (k t n) -> p k t n", k=2, t=T) for u in range(2)]
        n1_ps = [ps[:, (2 + u) * 1024:(3 + u) * 1024].rearrange("p (t c) -> p t c", t=T) for u in range(2)]
        n0_ps, n1T_ps, n1_ps = n0_ps * 2, n1T_ps * 2, n1_ps * 2

        s_w = sem("weights_loaded")
        s_all = sem("edge_arrays_loaded")
        s_fill = sem("weights_cleared")
        s_scaled = sem("weights_scaled")
        s_pconst = sem("pool_constants_made")
        s_step = sem("constants_step")
        s_zero = [sem(f"table{l}_zeroed") for l in range(2)]
        s_src = sem4("src_loaded")
        s_attr = sem4("attr_loaded")
        s_drow = sem4("dst_row_loaded")
        s_gather = sem4("rows_gathered")
        s_scat = sem2("sums_scattered")
        s_ptick = sem("pool_waited")
        s_sptick = sem("sp_waited")
        s_atick = sem("act_waited")
        s_dtick = sem("dve_waited")
        s_xgT = sem("xg_turned")
        s_xgTsb = sem("xg_turned_copied")
        s_hid = sem("hidden_done")
        s_hidsb = sem("hidden_copied")
        s_h = sem("h_done")
        s_hs = sem("h_copied")
        s_wd = sem("edge_weights_done")
        s_ea = sem("edge_attr_scaled")
        s_prod = sem("dot_products_ready")
        s_dot1 = sem("dot_first_sum")
        s_dot2 = sem("dot_second_sum")
        s_cross = sem("cross_difference")
        s_mid = sem("products_ready")
        s_midT = sem("products_turned")
        s_midTsb = sem("products_turned_copied")
        s_o = sem("second_map_done")
        s_ms = sem("message_scalars_ready")
        s_pe1 = sem("message_vector_part")
        s_mv = sem("message_vectors_ready")
        s_dstf = sem("dst_as_float")
        s_tsp = sem("spare_distance")
        s_same = sem("same_dst_ready")
        s_later = sem("later_edges_marked")
        s_stepd = sem("step_to_spare_row")
        s_row = sem("table_rows_ready")
        s_sum = sem("pair_summed")
        s_sumsb = sem("pair_sums_copied")

        s_nxT = sem4("turned_x_loaded")
        s_nx = sem4("node_inputs_loaded")
        s_z1 = sem("self_connection_added")
        s_nT = sem("nodes_turned")
        s_nTsb = sem("nodes_turned_copied")
        s_np = sem("self_connection_done")
        s_added = sem("table_row_added")
        s_pre = sem("preactivation_ready")
        s_gate = sem("gates_ready")
        s_f = sem("gated_ready")
        s_res = sem("residual_ready")
        s_bn = sem("stats_ready")
        s_p1, s_p2, s_p3, s_p4 = [sem(f"variance_step{n}") for n in range(4)]
        s_rstd = sem("rstd_ready")
        s_shift = sem("shift_ready")
        s_y = sem("y_ready")
        s_store = sem2("y_stored")
        s_q1 = sem("count_step1")
        s_q2 = sem("count_step2")
        s_q3 = sem("count_step3")
        s_q4 = sem("count_step4")

        loads = []
        for l, (w1, w2, l1s, l1v, scs, scv) in enumerate([
                ("L0_gnn_fc_w1", "L0_gnn_fc_w2", "L0_gnn_lin1_ws", "L0_gnn_lin1_wv", "L0_gnn_sc_ws", "L0_gnn_sc_wv"),
                ("L1_gnn_Wfc1", "L1_gnn_Wfc2", "L1_gnn_Wl1_0", "L1_gnn_Wl1_1", "L1_gnn_Wsc0", "L1_gnn_Wsc1")]):
            R = LAYERS[l]["R"]
            for t in range(2):
                loads.append((fc1[l][t * R:(t + 1) * R, t * H:(t + 1) * H], A[w1]))
                loads.append((fc2[l][t * H:(t + 1) * H, :], A[w2]))
            loads.append((lin1_s[l][:, :], A[l1s]))
            loads.append((self_s[l][:, :], A[scs]))
            for c in range(3):
                q = slice(c * V, (c + 1) * V)
                loads.append((lin1_v[l][q, q], A[l1v]))
                loads.append((self_v[l][q, q], A[scv]))
        ws, wv = A["L0_gnn_lin2_ws"], A["L0_gnn_lin2_wv"]
        loads.append((mapA[0][0:96, 0:96], ws))
        for c in range(3):
            loads.append((mapC[c * V:(c + 1) * V, c * V:(c + 1) * V], wv[96:128, :]))
        ws, wv1 = A["L1_gnn_Wl2_s"], A["L1_gnn_Wl2_v"]
        loads.append((mapA[1][0:96, 0:1], A["L1_gnn_Wa"]))
        loads.append((mapA[1][0:96, 1:65], ws))
        for l, w in ((0, wv), (1, wv1)):
            SO = LAYERS[l]["SO"]
            loads.append((mapA[l][96:128, SO:SO + V], w[64:96, :]))
            loads.append((mapB[l][0:32, 0:32], w[64:96, :]))
            loads.append((mapB[l][32:64, 32:64], w[64:96, :]))
            loads.append((mapB[l][64:128, 64:96], w[0:64, :]))

        i96 = 1 / math.sqrt(96.0)
        scales = [
            (fc1[0][:, :], 1 / 8), (fc1[1][:, :], 1 / 4),
            (fc2[0][:, 0:160], 1 / 8), (fc2[0][:, 160:192], 1 / 8 / math.sqrt(3.0)),
            (fc2[0][:, 192:224], 1 / 8 / math.sqrt(2.0)),
            (fc2[1][:, 0:160], 1 / 8), (fc2[1][:, 160:192], 1 / 8 / math.sqrt(3.0)),
            (mapA[0][:, 0:96], i96 / 4), (mapA[0][:, 96:128], 1 / math.sqrt(128.0) / 4),
            (mapB[0][:, :], 1 / math.sqrt(128.0) / 4), (mapC[:, :], 1 / math.sqrt(128.0) / 4),
            (mapA[1][:, :], i96), (mapB[1][:, :], i96)]
        for l in range(2):
            scales += [(lin1_s[l][:, :], 1 / 8), (self_s[l][:, :], 1 / 8),
                       (lin1_v[l][:, :], 1 / math.sqrt(32.0)), (self_v[l][:, :], 1 / math.sqrt(32.0))]
        cleared = [fc1[0], fc1[1], lin1_v[0], lin1_v[1], self_v[0], self_v[1],
                   mapA[0], mapA[1], mapB[0], mapB[1], mapC]

        block = ctx.enter_context(nc.Block())

        @block.sync
        def _(sp):
            sp.dma_start(dst_all[:, :], A["dst_col"]).then_inc(s_all, 16)
            sp.dma_start(attr_all[:, :, :].rearrange("p a b -> p (a b)"), A["attr6"]).then_inc(s_all, 16)
            sp.dma_start(a_all[:, :, :].rearrange("p g t -> p (g t)"), A["a_node"]).then_inc(s_all, 16)
            sp.wait_ge(s_fill, 1)
            for dst, src in loads:
                sp.dma_start(dst, src).then_inc(s_w, 16)

            for l in range(2):
                base = l * NP

                def load_src(j, m, u):
                    wait_count(sp, s_gather[u], landed(j - 4, u, 4, 32))
                    sp.dma_start(src_i[u][:, :], A["src_col"][bass.ds(m, 1)].rearrange("a p t -> p (a t)")).then_inc(s_src[u], 16)

                def load_attr(j, m, u):
                    wait_count(sp, s_hid, j - 3)
                    R2 = 2 * LAYERS[l]["R"]
                    sp.dma_start(attrT[u][0:R2, :], A[f"attrT{l}"][bass.ds(m, 1)].rearrange("a k e -> k (a e)")).then_inc(s_attr[u], 16)

                def load_dst_row(j, m, u):
                    wait_count(sp, s_same, j - 3)
                    sp.dma_start(dst_row[u][:, :], A["dst_row"][bass.ds(m, 1), :].partition_broadcast(P)).then_inc(s_drow[u], 16)

                run_stages(sp, base, NP, 10, [(0, load_src), (0, load_attr), (4, load_dst_row)])

                for u in range(2):
                    sp.wait_ge(s_scat[u], (l + 1) * NP * 16)

                def load_turned(g, m, u):
                    wait_count(sp, s_np, g - 3)
                    sp.dma_start(xsT[u][:, :], A["xsT"][bass.ds(m, 1)].rearrange("a k n -> k (a n)")).then_inc(s_nxT[u], 16)
                    sp.dma_start(xvT[u][:, :], A["xvT"][bass.ds(m, 1)].rearrange("a k n -> k (a n)")).then_inc(s_nxT[u], 16)

                def load_nodes(g, m, u):
                    wait_count(sp, s_res, g - 3)
                    sp.sem_inc(s_sptick, 1)
                    W = LAYERS[l]["ROW"]
                    if l == 1:
                        sp.dma_start(x1g[u][:, :, :].rearrange("p t c -> p (t c)"),
                                     x1_rows[bass.ds(m * GROUP, GROUP), :].rearrange("(p t) c -> p (t c)", t=T)).then_inc(s_nx[u], 16)
                    sp.dma_start(tab[u][:, :, :].rearrange("p t c -> p (t c)")[:, 0:T * W],
                                 table[l][bass.ds(m * GROUP, GROUP), :].rearrange("(p t) c -> p (t c)", t=T)).then_inc(s_nx[u], 16 * (2 - l))

                def clear_table1(g, m, u):
                    sp.dma_start(table[1][bass.ds(m * GROUP, GROUP), :].rearrange("(p t) c -> p (t c)", t=T),
                                 zeros[:, 0:T * LAYERS[1]["ROW"]]).then_inc(s_zero[1], 16)

                if l == 0:
                    sp.dma_start(table[1][N_PAD:ROWS, :].rearrange("(p t) c -> p (t c)", p=P),
                                 zeros[:, 0:2 * LAYERS[1]["ROW"]]).then_inc(s_zero[1], 16)
                    run_stages(sp, 0, NG, 6, [(0, load_turned), (0, load_nodes), (0, clear_table1)])
                else:
                    run_stages(sp, NG, NG, 6, [(0, load_nodes)])
                for u in range(2):
                    sp.wait_ge(s_store[u], (l + 1) * NG * 8)

        @block.gpsimd
        def _(pool):
            nc.gpsimd.memset(ident[:, :], 0.0)
            nc.gpsimd.memset(earlier[:, :], 1.0)
            nc.gpsimd.memset(minus_half[:, :], -0.5)
            nc.gpsimd.memset(quarter[:, :], 0.25)
            nc.gpsimd.iota(spare_i[:, :, :], pattern=[[0, NP], [P, 2]], base=N_PAD, channel_multiplier=1).then_inc(s_step, 1)
            pool.wait_ge(s_step, 1)
            nc.gpsimd.affine_select(out=ident[:, :], in_=ident[:, :], compare_op=ALU.not_equal, fill=1.0,
                                    base=0, pattern=[[-1, P]], channel_multiplier=1)
            nc.gpsimd.affine_select(out=earlier[:, P:PAIR], in_=earlier[:, P:PAIR], compare_op=ALU.is_gt, fill=0.0,
                                    base=0, pattern=[[-1, P]], channel_multiplier=1)
            nc.gpsimd.tensor_copy(spare_row[:, :, :], spare_i[:, :, :]).then_inc(s_pconst, 1)
            for l in range(2):
                rows, width = (A["x_rows"], D + 1) if l == 0 else (x1_rows, D)

                def gather(j, m, u):
                    wait_count(pool, s_xgT, j - 3)
                    if l == 0:
                        wait_count(pool, s_ea, j - 3)
                    pool.wait_ge(s_src[u], landed(j, u, 4))
                    pool.sem_inc(s_ptick, 1)
                    for t in range(2):
                        pool.indirect_dma_start(
                            out=xg[u][:, t, 0:width], out_offset=None, in_=rows,
                            in_offset=bass.IndirectOffsetOnAxis(ap=src_i[u][:, t:t + 1], axis=0)).then_inc(s_gather[u], 16)

                def scatter(j, m, u):
                    wait_count(pool, s_sumsb, j + 1)
                    wait_count(pool, s_row, j + 1)
                    wait_count(pool, s_scat[(u + 1) % 2], landed(j - 1, (u + 1) % 2, 2, 32))
                    if isinstance(j, int) and j == l * NP:
                        pool.wait_ge(s_zero[l], 16 * (25 if l == 0 else NG + 1))
                    pool.sem_inc(s_ptick, 1)
                    W = LAYERS[l]["ROW"]
                    for t in range(2):
                        pool.indirect_dma_start(
                            out=table[l], out_offset=bass.IndirectOffsetOnAxis(ap=row_i[u][:, t:t + 1], axis=0),
                            in_=sums[u][:, t, 0:W], in_offset=None, compute_op=ALU.add).then_inc(s_scat[u], 16)

                if l == 1:
                    for u in range(2):
                        pool.wait_ge(s_store[u], NG * 8)
                run_stages(pool, l * NP, NP, 10, [(0, gather), (7, scatter)])

                def powers(g, m, u):
                    st = stats[u]
                    tt, ts = nc.gpsimd.tensor_tensor, nc.gpsimd.tensor_scalar
                    pool.wait_ge(s_bn, g + 1)
                    wait_count(pool, s_y, g - 3)
                    tt(mean2[:, :], st[:, :, 1], st[:, :, 4], ALU.add)
                    tt(apart[:, :], st[:, :, 1], st[:, :, 4], ALU.subtract)
                    tt(squares[:, :], st[:, :, 2], st[:, :, 5], ALU.add).then_inc(s_p1, 1)
                    pool.wait_ge(s_p1, g + 1)
                    tt(apart2[:, :], apart[:, :], apart[:, :], ALU.mult)
                    ts(neg_mean[:, :], mean2[:, :], -0.5, None, ALU.mult)
                    ts(var_in[:, :], squares[:, :], 1.0 / D, EPS, ALU.mult, ALU.add).then_inc(s_p2, 1)
                    pool.wait_ge(s_p2, g + 1)
                    tt(apart2[:, :], apart2[:, :], quarter[:, :], ALU.mult).then_inc(s_p3, 1)
                    pool.wait_ge(s_p3, g + 1)
                    tt(var_e[:, :], var_in[:, :], apart2[:, :], ALU.add).then_inc(s_p4, 1)
                    pool.wait_ge(s_p4, g + 1)
                    tt(rstd[u][:, :], var_e[:, :], minus_half[:, :], ALU.pow).then_inc(s_rstd, 1)
                    pool.wait_ge(s_rstd, g + 1)
                    tt(shift[u][:, :], neg_mean[:, :], rstd[u][:, :], ALU.mult).then_inc(s_shift, 1)

                run_stages(pool, l * NG, NG, 6, [(0, powers)])

        @block.tensor
        def _(pe):
            mm, turn = nc.tensor.matmul, nc.tensor.transpose
            pe.wait_ge(s_scaled, 1)
            pe.wait_ge(s_pconst, 1)
            for l in range(2):
                L = LAYERS[l]
                SO, R2 = L["SO"], 2 * L["R"]

                def turn_x(j, m, u):
                    pe.wait_ge(s_gather[u], landed(j, u, 4, 32))
                    wait_count(pe, s_xgTsb, j)
                    for t in range(2):
                        turn(xgT_ps[0:96, 2 + t, :], xg[u][:, t, S:D], ident[:, :])
                        last = turn(xgT_ps[0:S, t, :], xg[u][:, t, 0:S], ident[:, :])
                    last.then_inc(s_xgT, 1)

                def hidden(j, m, u):
                    pe.wait_ge(s_attr[u], landed(j, u, 4))
                    wait_count(pe, s_hidsb, j)
                    mm(hidT_ps, fc1[l][0:R2, :], attrT[u][0:R2, :], start=True, stop=True).then_inc(s_hid, 1)

                def first_map(j, m, u):
                    pe.wait_ge(s_xgTsb, j + 1)
                    wait_count(pe, s_hs, j)
                    pe.wait_ge(s_hidsb, j + 1)
                    for t in range(2):
                        mm(h_ps[:, t, 0:S], xgT[u][0:S, t, :], lin1_s[l][:, :], start=True, stop=True)
                        last = mm(h_ps[:, t, S:D], xgT[u][0:96, 2 + t, :], lin1_v[l][:, :], start=True, stop=True)
                    last.then_inc(s_h, 1)

                def edge_weights(j, m, u):
                    wait_count(pe, s_mid, j)
                    for t in range(2):
                        q = slice(t * H, (t + 1) * H)
                        last = mm(w_ps[l][:, t, :], hidT[u][q, :], fc2[l][q, :], start=True, stop=True)
                    last.then_inc(s_wd, 1)

                def turn_mid(j, m, u):
                    pe.wait_ge(s_mid, j + 1)
                    wait_count(pe, s_midTsb, j)
                    for c in range(2):
                        for t in range(2):
                            last = turn(midT_ps[:, 2 * c + t, :], mid[u][:, t, c * P:(c + 1) * P], ident[:, :])
                    if L["cross"]:
                        for t in range(2):
                            last = turn(midT_ps[0:96, 4 + t, :], mid[u][:, t, 256:352], ident[:, :])
                    last.then_inc(s_midT, 1)

                def second_map(j, m, u):
                    pe.wait_ge(s_midTsb, j + 1)
                    wait_count(pe, s_ms, j)
                    wait_count(pe, s_mv, j)
                    for t in range(2):
                        mm(o_ps[l][:, t, 0:SO + V], midT[u][:, t, :], mapA[l][:, :], start=t == 0, stop=not L["cross"],
                           skip_group_check=True)
                        last = mm(o_ps[l][:, t, SO + V:SO + 4 * V], midT[u][:, 2 + t, :], mapB[l][:, :], start=False,
                                  stop=not L["cross"], skip_group_check=True)
                        if L["cross"]:
                            last = mm(o_ps[l][:, t, SO:SO + 3 * V], midT[u][0:96, 4 + t, :], mapC[:, :], start=False,
                                      stop=True, skip_group_check=True)
                    last.then_inc(s_o, 1)

                def sum_pair(j, m, u):
                    pe.wait_ge(s_ms, j + 1)
                    pe.wait_ge(s_mv, j + 1)
                    pe.wait_ge(s_same, j + 1)
                    wait_count(pe, s_sumsb, j)
                    mm(sum_ps[l][:, 0, :], same0[u][:, :], msg[l][u][:, 0, :], start=True, stop=False)
                    mm(sum_ps[l][:, 0, :], same1[u][:, 0:P], msg[l][u][:, 1, :], start=False, stop=True)
                    mm(sum_ps[l][:, 1, :], same1[u][:, P:PAIR], msg[l][u][:, 1, :], start=True, stop=True).then_inc(s_sum, 1)

                if l == 1:
                    pe.wait_ge(s_res, NG)
                run_stages(pe, l * NP, NP, 10, [(1, first_map), (0, hidden), (1, edge_weights), (0, turn_x),
                                                (3, second_map), (2, turn_mid), (5, sum_pair)])

                def nodes0(g, m, u):
                    pe.wait_ge(s_nxT[u], landed(g, u, 4, 32))
                    wait_count(pe, s_res, g - 1)
                    for t in range(T):
                        q = slice(t * P, (t + 1) * P)
                        o = n0_ps[u][:, t, :]
                        turn(o[:, 256:352], xvT[u][:, q], ident[0:96, 0:96])
                        turn(o[:, 192:256], xsT[u][:, q], ident[0:S, 0:S])
                        mm(o[:, 96:192], xvT[u][:, q], self_v[0][:, :], start=True, stop=True)
                        last = mm(o[:, 0:96], xsT[u][:, q], self_s[0][:, :], start=True, stop=True)
                    last.then_inc(s_np, 1)

                def turn1(g, m, u):
                    pe.wait_ge(s_nx[u], landed(g, u, 4, 32))
                    wait_count(pe, s_nTsb, g - 1 - NG)
                    for t in range(T):
                        turn(n1T_ps[u][0:96, 1, t, :], x1g[u][:, t, S:D], ident[:, :])
                        last = turn(n1T_ps[u][0:S, 0, t, :], x1g[u][:, t, 0:S], ident[:, :])
                    last.then_inc(s_nT, 1)

                def nodes1(g, m, u):
                    pe.wait_ge(s_nTsb, g + 1 - NG)
                    wait_count(pe, s_res, g - 1)
                    for t in range(T):
                        q = slice(t * P, (t + 1) * P)
                        o = n1_ps[u]
                        mm(o[:, t, 0:S], xsT[u][:, q], self_s[1][:, :], start=True, stop=True)
                        last = mm(o[:, t, S:D], xvT[u][:, q], self_v[1][:, :], start=True, stop=True)
                    last.then_inc(s_np, 1)

                pe.wait_ge(s_sumsb, (l + 1) * NP)
                if l == 0:
                    run_stages(pe, 0, NG, 6, [(0, nodes0)])
                else:
                    run_stages(pe, NG, NG, 6, [(0, turn1), (1, nodes1)])

        @block.scalar
        def _(act):
            copy = nc.scalar.copy
            act.wait_ge(s_w, 16 * len(loads))
            W0 = LAYERS[0]["ROW"]
            for k in range(25):
                n = min(2048, ROWS - k * 2048)
                act.dma_start(table[0][k * 2048:k * 2048 + n, :].rearrange("(p r) c -> p (r c)", p=P),
                              zeros[:, 0:n // P * W0]).then_inc(s_zero[0], 16)
            for l in range(2):
                L = LAYERS[l]
                SO, W = L["SO"], L["ROW"]

                def copy_h(j, m, u):
                    act.wait_ge(s_h, j + 1)
                    if not (isinstance(j, int) and j == (l + 1) * NP - 1):
                        act.wait_ge(s_hid, j + 2)
                    wait_count(act, s_mid, j - 1)
                    copy(hs[u][:, :, 0:D], h_ps[:, :, :])
                    copy(hs[u][:, :, D:D + 2 * V], h_ps[:, :, S:S + 2 * V]).then_inc(s_hs, 1)

                def hidden_act(j, m, u):
                    act.wait_ge(s_hid, j + 1)
                    wait_count(act, s_wd, j - 1)
                    nc.scalar.activation(hidT[u][:, :], hidT_ps, ACT.Silu).then_inc(s_hidsb, 1)

                def copy_xT(j, m, u):
                    act.wait_ge(s_xgT, j + 1)
                    wait_count(act, s_h, j - 1)
                    copy(xgT[u][0:S, 0:2, :], xgT_ps[0:S, 0:2, :])
                    copy(xgT[u][0:96, 2:4, :], xgT_ps[0:96, 2:4, :]).then_inc(s_xgTsb, 1)

                def copy_message(j, m, u):
                    act.wait_ge(s_o, j + 1)
                    wait_count(act, s_sum, j - 1)
                    copy(msg[l][u][:, :, 0:SO], o_ps[l][:, :, 0:SO]).then_inc(s_ms, 1)

                def copy_midT(j, m, u):
                    act.wait_ge(s_midT, j + 1)
                    wait_count(act, s_o, j - 1)
                    last = copy(midT[u][:, 0:4, :], midT_ps[:, 0:4, :])
                    if L["cross"]:
                        last = copy(midT[u][0:96, 4:6, :], midT_ps[0:96, 4:6, :])
                    last.then_inc(s_midTsb, 1)

                def copy_sums(j, m, u):
                    act.wait_ge(s_sum, j + 1)
                    wait_count(act, s_scat[u], landed(j - 2, u % 2, 2, 32))
                    copy(sums[u][:, :, 0:W], sum_ps[l][:, :, :]).then_inc(s_sumsb, 1)

                run_stages(act, l * NP, NP, 10, [(1, copy_h), (0, hidden_act), (0, copy_xT),
                                                 (3, copy_message), (2, copy_midT), (5, copy_sums)])

                def gates(g, m, u):
                    act.wait_ge(s_pre, g + 1)
                    wait_count(act, s_f, g - 1)
                    nc.scalar.activation(gate[u][:, :, :], pre[u][:, :, 0:96], ACT.Sigmoid).then_inc(s_gate, 1)

                def copy_nT(g, m, u):
                    act.wait_ge(s_nT, g + 1 - NG)
                    wait_count(act, s_np, g - 1)
                    copy(xsT[u][:, :].rearrange("p (t n) -> p t n", t=T), n1T_ps[u][0:S, 0, :, :])
                    copy(xvT[u][:, :].rearrange("p (t n) -> p t n", t=T), n1T_ps[u][0:96, 1, :, :]).then_inc(s_nTsb, 1)

                def normalise(g, m, u):
                    act.wait_ge(s_shift, g + 1)
                    wait_count(act, s_store[u], landed(g - 2, u % 2, 2))
                    for t in range(T):
                        last = nc.scalar.activation(y[u][:, t, :], res[u][:, t, :], ACT.Identity,
                                                    scale=rstd[u][:, t:t + 1], bias=shift[u][:, t:t + 1])
                    last.then_inc(s_y, 1)

                def store(g, m, u):
                    act.wait_ge(s_y, g + 1)
                    act.sem_inc(s_atick, 1)
                    to = x1_rows if l == 0 else out
                    act.dma_start(to[bass.ds(m * GROUP, GROUP), :].rearrange("(p t) c -> p (t c)", t=T),
                                  y[u][:, :, :].rearrange("p t c -> p (t c)")).then_inc(s_store[u], 16)

                run_stages(act, l * NG, NG, 6, [(0, gates if l == 0 else copy_nT), (4, store), (3, normalise)])

        @block.vector
        def _(dve):
            tt, stt = nc.vector.tensor_tensor, nc.vector.scalar_tensor_tensor
            for w in cleared:
                nc.vector.memset(w[:, :], 0.0)
            for u in range(2):
                nc.vector.memset(msg[1][u][:, :, 161:162], 1.0)
            nc.vector.memset(zeros[:, :], 0.0).then_inc(s_fill, 1)
            dve.wait_ge(s_w, 16 * len(loads))
            dve.wait_ge(s_fill, 1)
            for w, f in scales:
                last = nc.vector.tensor_scalar(w, w, f, None, ALU.mult)
            last.then_inc(s_scaled, 1)
            dve.wait_ge(s_all, 48)
            dve.wait_ge(s_pconst, 1)
            nc.vector.tensor_copy(dst_f[:, :], dst_all[:, :]).then_inc(s_dstf, 1)
            dve.wait_ge(s_dstf, 1)
            tt(to_spare[:, :], spare_row[:, :, :].rearrange("p j t -> p (j t)"), dst_f[:, :], ALU.subtract).then_inc(s_tsp, 1)
            dve.wait_ge(s_tsp, 1)

            def planes(ap):
                return ap.rearrange("p t (i c) -> p t i c", c=V)

            for l in range(2):
                L = LAYERS[l]
                SO = L["SO"]

                def scale_attr(j, m, u):
                    dve.wait_ge(s_gather[u], landed(j, u, 4, 32))
                    at = bass.ds(m * 2, 2)
                    a = xg[u][:, :, D:D + 1].to_broadcast([P, 2, 6])
                    tt(ea_all[:, at, :], attr_all[:, at, :], a, ALU.mult).then_inc(s_ea, 1)

                def products(j, m, u):
                    dve.wait_ge(s_hs, j + 1)
                    if l == 0:
                        dve.wait_ge(s_ea, j + 1)
                    wait_count(dve, s_midT, j - 1)
                    h, w, o = hs[u], w_ps[l], mid[u]
                    hv = h[:, :, S:D + 2 * V].rearrange("p t (i c) -> p t i c", c=V)

                    def comp(k):
                        return ea_all[:, bass.ds(m * 2, 2), k:k + 3].unsqueeze(3).to_broadcast([P, 2, 3, V])

                    def e0(t):
                        return ea_all[:, bass.ds(m * 2 + t, 1), 0:1].rearrange("p a b -> p (a b)")

                    tt(planes(prod[u][:, :, :]), hv[:, :, 0:3, :], comp(1), ALU.mult).then_inc(s_prod, 1)
                    if L["cross"]:
                        tt(planes(crossA[u][:, :, :]), hv[:, :, 1:4, :], comp(3), ALU.mult)
                        tt(planes(crossB[u][:, :, :]), hv[:, :, 2:5, :], comp(2), ALU.mult)
                    dve.wait_ge(s_prod, j + 1)
                    last = tt(dot[u][:, :, :], prod[u][:, :, 0:V], prod[u][:, :, V:2 * V], ALU.add)
                    last.then_inc(s_dot1, 1)
                    dve.wait_ge(s_wd, j + 1)
                    tt(o[:, :, 192:256], h[:, :, 0:S], w[:, :, 64:128], ALU.mult)
                    for t in range(2):
                        stt(o[:, t, 0:S], h[:, t, 0:S], e0(t), w[:, t, 0:S], ALU.mult, ALU.mult)
                    dve.wait_ge(s_dot1, j + 1)
                    tt(dot[u][:, :, :], dot[u][:, :, :], prod[u][:, :, 2 * V:3 * V], ALU.add).then_inc(s_dot2, 1)
                    if L["cross"]:
                        tt(crossA[u][:, :, :], crossA[u][:, :, :], crossB[u][:, :, :], ALU.subtract).then_inc(s_cross, 1)
                    for t in range(2):
                        stt(o[:, t, 96:192].rearrange("p (i c) -> p i c", c=V), hv[:, t, 0:3, :], e0(t),
                            w[:, t:t + 1, 128:160].to_broadcast([P, 3, V]), ALU.mult, ALU.mult)
                    dve.wait_ge(s_dot2, j + 1)
                    last = tt(o[:, :, S:S + V], dot[u][:, :, :], w[:, :, 160:192], ALU.mult)
                    if L["cross"]:
                        dve.wait_ge(s_cross, j + 1)
                        last = tt(planes(o[:, :, 256:352]), planes(crossA[u][:, :, :]),
                                  w[:, :, 192:224].unsqueeze(2).to_broadcast([P, 2, 3, V]), ALU.mult)
                    last.then_inc(s_mid, 1)

                def message_vectors(j, m, u):
                    dve.wait_ge(s_ms, j + 1)
                    wait_count(dve, s_sum, j - 1)
                    e1 = ea_all[:, bass.ds(m * 2, 2), 1:4].unsqueeze(3).to_broadcast([P, 2, 3, V])
                    p32 = o_ps[l][:, :, SO + 3 * V:SO + 4 * V].unsqueeze(2).to_broadcast([P, 2, 3, V])
                    tt(planes(pe1[u][:, :, :]), p32, e1, ALU.mult).then_inc(s_pe1, 1)

                def message_sum(j, m, u):
                    dve.wait_ge(s_pe1, j + 1)
                    tt(msg[l][u][:, :, SO:SO + 3 * V], pe1[u][:, :, :], o_ps[l][:, :, SO:SO + 3 * V], ALU.add).then_inc(s_mv, 1)

                def compare(j, m, u):
                    dve.wait_ge(s_drow[u], landed(j, u, 4))
                    wait_count(dve, s_sum, j - 1)

                    def dst(t):
                        return dst_f[:, bass.ds(m * 2 + t, 1)]

                    nc.vector.tensor_scalar(same0[u][:, :], dst_row[u][:, 0:P], dst(0), None, ALU.is_equal)
                    nc.vector.tensor_scalar(same1[u][:, :], dst_row[u][:, :], dst(1), None, ALU.is_equal).then_inc(s_same, 1)

                def mark_later(j, m, u):
                    dve.wait_ge(s_same, j + 1)
                    dve.sem_inc(s_dtick, 1)
                    ttr = nc.vector.tensor_tensor_reduce
                    ttr(out=junk[:, 0:P], in0=same0[u][:, :], in1=earlier[:, P:PAIR], scale=1.0, scalar=0.0,
                        op0=ALU.mult, op1=ALU.max, accum_out=is_later[u][:, 0:1])
                    ttr(out=junk[:, P:], in0=same1[u][:, :], in1=earlier[:, :], scale=1.0, scalar=0.0,
                        op0=ALU.mult, op1=ALU.max, accum_out=is_later[u][:, 1:2]).then_inc(s_later, 1)

                def step_rows(j, m, u):
                    dve.wait_ge(s_later, j + 1)
                    tt(step[u][:, :], is_later[u][:, :], to_spare[:, bass.ds(m * 2, 2)], ALU.mult).then_inc(s_stepd, 1)

                def choose_rows(j, m, u):
                    wait_count(dve, s_scat[u], landed(j - 2, u % 2, 2, 32))
                    at = bass.ds(m * 2, 2)
                    if l == 0:
                        dve.wait_ge(s_stepd, j + 1)
                        tt(row_i[u][:, :], step[u][:, :], dst_f[:, at], ALU.add)
                        tt(row_all[:, at], step[u][:, :], dst_f[:, at], ALU.add).then_inc(s_row, 1)
                    else:
                        nc.vector.tensor_copy(row_i[u][:, :], row_all[:, at]).then_inc(s_row, 1)

                if l == 0:
                    run_stages(dve, 0, NP, 10, [
                        (4, message_vectors), (0, scale_attr), (4, compare), (4, message_sum), (4, mark_later),
                        (1, products), (4, step_rows), (5, choose_rows)])
                else:
                    run_stages(dve, NP, NP, 10, [
                        (4, message_vectors), (4, compare), (4, message_sum), (1, products), (5, choose_rows)])

                def add_table(g, m, u):
                    dve.wait_ge(s_np, g + 1)
                    dve.wait_ge(s_nx[u], landed(g, u, 4, 32))
                    wait_count(dve, s_gate, g - 1)
                    tt(pre[u][:, :, :], n0_ps[u][:, :, 0:192], tab[u][:, :, :], ALU.add).then_inc(s_added, 1)

                def scale_pre(g, m, u):
                    dve.wait_ge(s_added, g + 1)
                    a = a_all[:, bass.ds(m, 1), :].rearrange("p g t -> p (g t)").unsqueeze(2).to_broadcast([P, T, 192])
                    tt(pre[u][:, :, :], pre[u][:, :, :], a, ALU.mult).then_inc(s_pre, 1)

                def gated0(g, m, u):
                    dve.wait_ge(s_gate, g + 1)
                    wait_count(dve, s_y, g - 3)
                    tt(res[u][:, :, 0:S], pre[u][:, :, 0:S], gate[u][:, :, 0:S], ALU.mult)
                    tt(planes(res[u][:, :, S:D]), planes(pre[u][:, :, 96:192]),
                       gate[u][:, :, S:96].unsqueeze(2).to_broadcast([P, T, 3, V]), ALU.mult).then_inc(s_f, 1)

                def residual0(g, m, u):
                    dve.wait_ge(s_f, g + 1)
                    tt(res[u][:, :, :], res[u][:, :, :], n0_ps[u][:, :, 192:352], ALU.add).then_inc(s_res, 1)

                W = LAYERS[1]["ROW"]
                tab1 = [t_[:, :, :].rearrange("p t c -> p (t c)")[:, 0:T * W].rearrange("p (t c) -> p t c", c=W) for t_ in tab]

                def residual1(g, m, u):
                    tb, q = tab1[u], small[u]
                    a_of = a_all[:, bass.ds(m, 1), :].rearrange("p g t -> p (g t)")
                    dve.wait_ge(s_nx[u], landed(g, u, 4, 32))
                    nc.vector.tensor_scalar(q[:, :, 0], tb[:, :, 161], 1.0, None, ALU.max).then_inc(s_q1, 1)
                    dve.wait_ge(s_np, g + 1)
                    wait_count(dve, s_y, g - 3)

                    def self_connection(t):
                        a = a_all[:, bass.ds(m, 1), t:t + 1].rearrange("p g t -> p (g t)")
                        return stt(res[u][:, t, :], n1_ps[u][:, t, 0:D], a, x1g[u][:, t, :], ALU.mult, ALU.add)

                    self_connection(0)
                    dve.wait_ge(s_q1, g + 1 - NG)
                    nc.vector.reciprocal(q[:, :, 1], q[:, :, 0]).then_inc(s_q2, 1)
                    self_connection(1)
                    dve.wait_ge(s_q2, g + 1 - NG)
                    tt(q[:, :, 2], q[:, :, 1], a_of, ALU.mult).then_inc(s_q3, 1)
                    self_connection(2)
                    dve.wait_ge(s_q3, g + 1 - NG)
                    tt(q[:, :, 3], q[:, :, 2], q[:, :, 2], ALU.mult).then_inc(s_q4, 1)
                    self_connection(3).then_inc(s_z1, 1)
                    dve.wait_ge(s_q4, g + 1 - NG)
                    tt(q[:, :, 0], q[:, :, 3], tb[:, :, 0], ALU.mult).then_inc(s_f, 1)

                def table_row1(g, m, u):
                    dve.wait_ge(s_z1, g + 1 - NG)
                    dve.wait_ge(s_f, g + 1)
                    for t in range(T):
                        last = stt(res[u][:, t, :], tab1[u][:, t, 1:161], small[u][:, t, 0:1], res[u][:, t, :], ALU.mult, ALU.add)
                    last.then_inc(s_res, 1)

                def stats_of(g, m, u):
                    dve.wait_ge(s_res, g + 1)
                    wait_count(dve, s_shift, g - 1)
                    for t in range(T):
                        last = nc.vector.bn_stats(stats[u][:, t, :], res[u][:, t, :])
                    last.then_inc(s_bn, 1)

                if l == 0:
                    run_stages(dve, 0, NG, 6, [(1, gated0), (1, residual0), (0, add_table), (0, scale_pre), (2, stats_of)])
                else:
                    run_stages(dve, NG, NG, 6, [(0, residual1), (1, stats_of), (0, table_row1)])


_WEIGHTS = [
    "L0_gnn_lin1_ws", "L0_gnn_lin1_wv", "L0_gnn_fc_w1", "L0_gnn_fc_w2", "L0_gnn_sc_ws", "L0_gnn_sc_wv",
    "L0_gnn_lin2_ws", "L0_gnn_lin2_wv", "L1_gnn_Wfc1", "L1_gnn_Wfc2", "L1_gnn_Wsc0", "L1_gnn_Wsc1",
    "L1_gnn_Wl1_0", "L1_gnn_Wl1_1", "L1_gnn_Wl2_s", "L1_gnn_Wl2_v", "L1_gnn_Wa"]


def kernel(**inputs):
    import concourse.bacc as bacc
    from concourse.bass_utils import run_bass_kernel_spmd

    g = {k: np.asarray(v) for k, v in inputs.items()}
    x, a = g["x"], g["node_vec1"]
    planar = np.concatenate([x[:, :S], x[:, S:].reshape(N, V, 3).transpose(0, 2, 1).reshape(N, 3 * V)], 1)
    padded = np.zeros((N_PAD, D), x.dtype)
    padded[:N] = planar
    turned = padded.reshape(NG, P, T, D).transpose(0, 3, 2, 1).reshape(NG, D, GROUP)
    a_node = np.zeros(N_PAD, a.dtype)
    a_node[:N] = a[:, 0]

    def edges(v, fill=0):
        p = np.full((NP * PAIR,) + v.shape[1:], fill, v.dtype)
        p[:E] = v
        return p.reshape((NP, 2, P) + v.shape[1:])

    src, dst = edges(g["src"]), edges(g["dst"], N)
    attr = edges(g["edge_attr_4"])[..., [0, 1, 2, 3, 1, 2]]
    arrays = {
        "x_rows": np.concatenate([planar, a], 1),
        "xsT": turned[:, :S], "xvT": turned[:, S:],
        "a_node": a_node.reshape(NG, P, T).transpose(1, 0, 2).reshape(P, NG * T),
        "src_col": src.transpose(0, 2, 1),
        "dst_col": dst.transpose(2, 0, 1).reshape(P, NP * 2),
        "dst_row": dst.reshape(NP, PAIR),
        "attr6": attr.transpose(2, 0, 1, 3).reshape(P, NP * 12),
        "attrT0": edges(g["edge_attr_64"]).transpose(0, 1, 3, 2).reshape(NP, 128, P),
        "attrT1": edges(g["edge_attr_16"]).transpose(0, 1, 3, 2).reshape(NP, 32, P),
        **{k: g[k] for k in _WEIGHTS},
    }
    arrays = {f"in_{k}": np.ascontiguousarray(v) for k, v in arrays.items()}
    nc = bacc.Bacc("TRN2", target_bir_lowering=False, num_devices=1)
    aps = {k[3:]: nc.dram_tensor(k, v.shape, mybir.dt.from_np(v.dtype), kind="ExternalInput").ap()
           for k, v in arrays.items()}
    out = nc.dram_tensor("out_rows", (N_PAD, D), F32, kind="ExternalOutput").ap()
    program(nc, aps, out)
    r = run_bass_kernel_spmd(nc, [arrays], core_ids=[0]).results[0]["out_rows"]
    r = np.asarray(r)[:N]
    return np.concatenate([r[:, :S], r[:, S:].reshape(N, 3, V).transpose(0, 2, 1).reshape(N, 3 * V)], 1)
```

```python
import math

import numpy as np
import concourse.bass as bass
from concourse import mybir
from contextlib import ExitStack

F32 = mybir.dt.float32
I32 = mybir.dt.int32
ALU = mybir.AluOpType
ACT = mybir.ActivationFunctionType

P = 128
N, E = 50000, 25000
S, V = 64, 32
D = S + 3 * V
M = S + 2 * V
PAIR = 2 * P
NP = -(-E // PAIR)
T = 4
GROUP = T * P
NG = -(-N // GROUP)
N_PAD = NG * GROUP
ROWS = N_PAD + PAIR
H = 64
EPS = 1e-5
WARM = [6, 6]

LAYERS = [
    dict(R=64, W=224, SO=96, SG=96, ROW=192, cross=True),
    dict(R=16, W=192, SO=65, SG=64, ROW=162, cross=False),
]


def wait_count(eng, sem, n):
    if not isinstance(n, int) or n > 0:
        eng.wait_ge(sem, n)


def run_stages(eng, base, count, depth, stages):
    assert (count - depth) % 4 == 0
    for k in range(base, base + depth):
        for lag, f in stages:
            if k - lag >= base:
                f(k - lag, k - lag - base, (k - lag) % 4)
    with eng.Fori(base + depth, base + count - 3, 4) as i:
        for r in range(4):
            for lag, f in stages:
                f(i + (r - lag), i + (r - lag - base), (base + depth + r - lag) % 4)
    for k in range(base + count, base + count + depth):
        for lag, f in stages:
            if k - lag < base + count:
                f(k - lag, k - lag - base, (k - lag) % 4)


def landed(j, turn, ring, per=16):
    return (j - turn) * (per // ring) + per


def stored(n, turn):
    return 16 * len(range(turn, n, 4))


def program(nc, A, out):
    ctx = ExitStack()
    with ctx:
        def sb(name, shape, dt=F32):
            return ctx.enter_context(nc.sbuf_tensor(name, shape, dt))

        def two(name, shape, dt=F32):
            return [sb(f"{name}{u}", shape, dt) for u in range(2)] * 2

        def four(name, shape, dt=F32):
            return [sb(f"{name}{u}", shape, dt) for u in range(4)]

        def sem(name):
            return ctx.enter_context(nc.semaphore(name))

        def sem2(name):
            return [sem(f"{name}{u}") for u in range(2)] * 2

        def sem4(name):
            return [sem(f"{name}{u}") for u in range(4)]

        def dram(name, shape):
            return nc.dram_tensor(name, shape, F32, kind="Internal").ap()

        x1_rows = dram("x1_rows", (N_PAD, D))
        table = [dram(f"table{l}", (ROWS, LAYERS[l]["ROW"])) for l in range(2)]

        ident = sb("ident", [P, P])
        fc1 = [sb("fc1_0", [P, 2 * H]), sb("fc1_1", [32, 2 * H])]
        fc2 = [sb(f"fc2_{l}", [P, LAYERS[l]["W"]]) for l in range(2)]
        lin1_m = [sb(f"lin1_m{l}", [M, M]) for l in range(2)]
        lin1_z = [sb(f"lin1_z{l}", [2 * V, 2 * V]) for l in range(2)]
        mapA = [sb(f"mapA{l}", [P, LAYERS[l]["SO"] + V]) for l in range(2)]
        mapB = [sb(f"mapB{l}", [P, 3 * V]) for l in range(2)]
        mapC = sb("mapC", [3 * V, 3 * V])
        self_m = [sb(f"self_m{l}", [M, LAYERS[l]["SG"] + 2 * V]) for l in range(2)]
        self_z = [sb(f"self_z{l}", [T * V, T * V]) for l in range(2)]
        zeros = sb("zeros", [P, 16 * 192])
        earlier = sb("earlier", [P, PAIR])
        spare_row = sb("spare_row", [P, NP, 2])
        spare_i = sb("spare_i", [P, NP, 2], I32)
        minus_half = sb("minus_half", [P, T])
        quarter = sb("quarter", [P, T])

        dst_all = sb("dst_all", [P, NP * 2], I32)
        attr_all = sb("attr_all", [P, NP * 2, 6])
        ea_all = sb("ea_all", [P, NP * 2, 6])
        row_all = sb("row_all", [P, NP * 2], I32)
        dst_f = sb("dst_f", [P, NP * 2])
        to_spare = sb("to_spare", [P, NP * 2])
        a_all = sb("a_all", [P, NG, T])

        src_i = four("src_i", [P, 2], I32)
        xg = four("xg", [P, 2, D + 1])
        attrT = four("attrT", [P, P])
        dst_row = four("dst_row", [P, PAIR], I32)
        xgT = two("xgT", [P, 3, P])
        xz = two("xz", [P, 2, V])
        hidT = two("hidT", [P, P])
        hs = two("hs", [P, 2, D + 2 * V])
        mid = two("mid", [P, 2, 352])
        midT = two("midT", [P, 6, P])
        msg = [two(f"msg{l}_", [P, 2, LAYERS[l]["ROW"]]) for l in range(2)]
        pe1 = two("pe1", [P, 2, 3 * V])
        same0 = two("same0", [P, P])
        same1 = two("same1", [P, PAIR])
        sums = two("sums", [P, 2, 192])
        row_i = two("row_i", [P, 2], I32)
        prod = two("prod", [P, 2, 3 * V])
        crossA = two("crossA", [P, 2, 3 * V])
        crossB = two("crossB", [P, 2, 3 * V])
        dot = two("dot", [P, 2, V])
        is_later = two("is_later", [P, 2])
        step = two("step", [P, 2])
        junk = sb("junk", [P, 3 * P])

        xT = four("xT", [M, GROUP])
        zT = four("zT", [T * V, P])
        x1g = four("x1g", [P, T, D])
        x1z = two("x1z", [P, T, V])
        tab = four("tab", [P, T, 192])
        gate = two("gate", [P, T, 96])
        res = four("res", [P, T, D])
        stats = two("stats", [P, T, 6])
        mean2, apart, squares, apart2, var_in, var_e, neg_mean = [
            sb(n, [P, T]) for n in ("mean2", "apart", "squares", "apart2", "var_in", "var_e", "neg_mean")]
        rstd = four("rstd", [P, T])
        shift = four("shift", [P, T])
        y = four("y", [P, T, D])
        small = two("small", [P, T, 4])

        W1 = LAYERS[1]["ROW"]
        tab1 = [t_[:, :, :].rearrange("p t c -> p (t c)")[:, 0:T * W1].rearrange("p (t c) -> p t c", c=W1) for t_ in tab]

        ps = ctx.enter_context(nc.psum_tensor("ps", [P, 8 * 512], F32))

        def bank(b, n=512):
            return ps[:, b * 512:b * 512 + n]

        xgT_ps = bank(0, 384).rearrange("p (k e) -> p k e", k=3)
        hidT_ps = bank(1)[:, 384:512]
        h_ps = bank(1, 2 * D).rearrange("p (t c) -> p t c", t=2)
        w_ps = [ps[:, 1024:2048].rearrange("p (t c) -> p t c", t=2)[:, :, 0:L["W"]] for L in LAYERS]
        midT_ps = bank(4, 768).rearrange("p (k e) -> p k e", k=6)
        o_ps = [bank(6, 2 * (L["SO"] + 128)).rearrange("p (t c) -> p t c", t=2) for L in LAYERS]
        sum_ps = [bank(7, 2 * L["ROW"]).rearrange("p (t c) -> p t c", t=2) for L in LAYERS]
        n0_ps = [ps[:, u * 1024:(u + 1) * 1024].rearrange("p (b c) -> p b c", b=2)[:, :, 0:384]
                 .rearrange("p b (t c) -> p b t c", t=2) for u in range(2)]
        x0_ps = [bank(4 + 2 * u).rearrange("p (t c) -> p t c", t=T) for u in range(2)]
        z0_ps = [bank(5 + 2 * u, T * V).rearrange("p (t c) -> p t c", t=T) for u in range(2)]
        x1T_ps = [bank(2 * u) for u in range(2)]
        z1T_ps = [bank(2 * u + 1, P) for u in range(2)]
        n1_ps = [ps[:, (2 + u) * 1024:(3 + u) * 1024].rearrange("p (b c) -> p b c", b=2)[:, :, 0:2 * D]
                 .rearrange("p b (t c) -> p b t c", t=2) for u in range(2)]
        n0_ps, x0_ps, z0_ps, x1T_ps, z1T_ps, n1_ps = [b * 2 for b in (n0_ps, x0_ps, z0_ps, x1T_ps, z1T_ps, n1_ps)]

        s_w = sem("weights_loaded")
        s_all = sem("edge_arrays_loaded")
        s_fill = sem("weights_cleared")
        s_scaled = sem("weights_scaled")
        s_pconst = sem("pool_constants_made")
        s_step = sem("constants_step")
        s_zero = [sem(f"table{l}_zeroed") for l in range(2)]
        s_src = sem4("src_loaded")
        s_attr = sem4("attr_loaded")
        s_drow = sem4("dst_row_loaded")
        s_gather = sem4("rows_gathered")
        s_scat = sem2("sums_scattered")
        s_ptick = sem("pool_waited")
        s_sptick = sem("sp_waited")
        s_atick = sem("act_waited")
        s_dtick = sem("dve_waited")
        s_xz = sem("z_gathered_together")
        s_xgT = sem("xg_turned")
        s_xgTsb = sem("xg_turned_copied")
        s_hid = sem("hidden_done")
        s_hidsb = sem("hidden_copied")
        s_h = sem("h_done")
        s_hs = sem("h_copied")
        s_wd = sem("edge_weights_done")
        s_ea = sem("edge_attr_scaled")
        s_prod = sem("dot_products_ready")
        s_dot1 = sem("dot_first_sum")
        s_dot2 = sem("dot_second_sum")
        s_cross = sem("cross_difference")
        s_mid = sem("products_ready")
        s_midT = sem("products_turned")
        s_midTsb = sem("products_turned_copied")
        s_o = sem("second_map_done")
        s_ms = sem("message_scalars_ready")
        s_pe1 = sem("message_vector_part")
        s_mv = sem("message_vectors_ready")
        s_dstf = sem("dst_as_float")
        s_tsp = sem("spare_distance")
        s_same = sem("same_dst_ready")
        s_later = sem("later_edges_marked")
        s_stepd = sem("step_to_spare_row")
        s_row = sem("table_rows_ready")
        s_sum = sem("pair_summed")
        s_sumsb = sem("pair_sums_copied")

        s_nxT = sem4("turned_x_loaded")
        s_nx = sem4("node_inputs_loaded")
        s_z1 = sem("self_connection_added")
        s_nT = sem("nodes_turned")
        s_nTsb = sem("nodes_turned_copied")
        s_np = sem("self_connection_done")
        s_xb = sem("x_turned_back")
        s_added = sem("table_row_added")
        s_scgate = sem("gates_scaled")
        s_gate = sem("gates_ready")
        s_f = sem("gated_ready")
        s_res = sem("residual_ready")
        s_bn = sem("stats_ready")
        s_p1, s_p2, s_p3, s_p4 = [sem(f"variance_step{n}") for n in range(4)]
        s_rstd = sem("rstd_ready")
        s_shift = sem("shift_ready")
        s_y = sem("y_ready")
        s_store = sem4("y_stored")
        s_q1 = sem("count_step1")
        s_q2 = sem("count_step2")
        s_q3 = sem("count_step3")
        s_q4 = sem("count_step4")
        s_q5 = sem("factor_ready")

        loads = []
        for l, (w1, w2, l1s, l1v, scs, scv) in enumerate([
                ("L0_gnn_fc_w1", "L0_gnn_fc_w2", "L0_gnn_lin1_ws", "L0_gnn_lin1_wv", "L0_gnn_sc_ws", "L0_gnn_sc_wv"),
                ("L1_gnn_Wfc1", "L1_gnn_Wfc2", "L1_gnn_Wl1_0", "L1_gnn_Wl1_1", "L1_gnn_Wsc0", "L1_gnn_Wsc1")]):
            R = LAYERS[l]["R"]
            for t in range(2):
                loads.append((fc1[l][t * R:(t + 1) * R, t * H:(t + 1) * H], A[w1]))
                loads.append((fc2[l][t * H:(t + 1) * H, :], A[w2]))
            SG = LAYERS[l]["SG"]
            loads.append((lin1_m[l][0:S, 0:S], A[l1s]))
            loads.append((self_m[l][0:S, 0:SG], A[scs]))
            for c in range(2):
                q = slice(S + c * V, S + (c + 1) * V)
                loads.append((lin1_m[l][q, q], A[l1v]))
                loads.append((self_m[l][q, SG + c * V:SG + (c + 1) * V], A[scv]))
            for t in range(T):
                q = slice(t * V, (t + 1) * V)
                loads.append((self_z[l][q, q], A[scv]))
                if t < 2:
                    loads.append((lin1_z[l][q, q], A[l1v]))
        ws, wv = A["L0_gnn_lin2_ws"], A["L0_gnn_lin2_wv"]
        loads.append((mapA[0][0:96, 0:96], ws))
        for c in range(3):
            loads.append((mapC[c * V:(c + 1) * V, c * V:(c + 1) * V], wv[96:128, :]))
        ws, wv1 = A["L1_gnn_Wl2_s"], A["L1_gnn_Wl2_v"]
        loads.append((mapA[1][0:96, 0:1], A["L1_gnn_Wa"]))
        loads.append((mapA[1][0:96, 1:65], ws))
        for l, w in ((0, wv), (1, wv1)):
            SO = LAYERS[l]["SO"]
            loads.append((mapA[l][96:128, SO:SO + V], w[64:96, :]))
            loads.append((mapB[l][0:32, 0:32], w[64:96, :]))
            loads.append((mapB[l][32:64, 32:64], w[64:96, :]))
            loads.append((mapB[l][64:128, 64:96], w[0:64, :]))

        i96 = 1 / math.sqrt(96.0)
        scales = [
            (fc1[0][:, :], 1 / 8), (fc1[1][:, :], 1 / 4),
            (fc2[0][:, 0:160], 1 / 8), (fc2[0][:, 160:192], 1 / 8 / math.sqrt(3.0)),
            (fc2[0][:, 192:224], 1 / 8 / math.sqrt(2.0)),
            (fc2[1][:, 0:160], 1 / 8), (fc2[1][:, 160:192], 1 / 8 / math.sqrt(3.0)),
            (mapA[0][:, 0:96], i96 / 4), (mapA[0][:, 96:128], 1 / math.sqrt(128.0) / 4),
            (mapB[0][:, :], 1 / math.sqrt(128.0) / 4), (mapC[:, :], 1 / math.sqrt(128.0) / 4),
            (mapA[1][:, :], i96), (mapB[1][:, :], i96)]
        for l in range(2):
            SG = LAYERS[l]["SG"]
            v32 = 1 / math.sqrt(32.0)
            scales += [(lin1_m[l][:, 0:S], 1 / 8), (lin1_m[l][:, S:M], v32), (lin1_z[l][:, :], v32),
                       (self_m[l][:, 0:SG], 1 / 8), (self_m[l][:, SG:SG + 2 * V], v32), (self_z[l][:, :], v32)]
        cleared = [fc1[0], fc1[1], *lin1_m, *lin1_z, *self_m, *self_z,
                   mapA[0], mapA[1], mapB[0], mapB[1], mapC]

        block = ctx.enter_context(nc.Block())

        @block.sync
        def _(sp):
            sp.dma_start(dst_all[:, :], A["dst_col"]).then_inc(s_all, 16)
            sp.dma_start(attr_all[:, :, :].rearrange("p a b -> p (a b)"), A["attr6"]).then_inc(s_all, 16)
            sp.dma_start(a_all[:, :, :].rearrange("p g t -> p (g t)"), A["a_node"]).then_inc(s_all, 16)
            sp.wait_ge(s_fill, 1)
            for dst, src in loads:
                sp.dma_start(dst, src).then_inc(s_w, 16)

            for l in range(2):
                base = l * NP

                def load_src(j, m, u):
                    wait_count(sp, s_gather[u], landed(j - 4, u, 4, 32))
                    sp.dma_start(src_i[u][:, :], A["src_col"][bass.ds(m, 1)].rearrange("a p t -> p (a t)")).then_inc(s_src[u], 16)

                def load_attr(j, m, u):
                    wait_count(sp, s_hid, j - 3)
                    R2 = 2 * LAYERS[l]["R"]
                    sp.dma_start(attrT[u][0:R2, :], A[f"attrT{l}"][bass.ds(m, 1)].rearrange("a k e -> k (a e)")).then_inc(s_attr[u], 16)

                def load_dst_row(j, m, u):
                    wait_count(sp, s_same, j - 3)
                    sp.dma_start(dst_row[u][:, :], A["dst_row"][bass.ds(m, 1), :].partition_broadcast(P)).then_inc(s_drow[u], 16)

                def clear_table1(j, m, u):
                    sp.dma_start(table[1][bass.ds(m * GROUP, GROUP), :].rearrange("(p t) c -> p (t c)", t=T),
                                 zeros[:, 0:T * LAYERS[1]["ROW"]]).then_inc(s_zero[1], 16)

                assert NP == NG
                run_stages(sp, base, NP, 10, [(0, load_src), (0, load_attr), (4, load_dst_row)] + [(4, clear_table1)] * (l == 0))

                W = LAYERS[l]["ROW"]

                def load_turned(g, m, u):
                    wait_count(sp, s_xb, g - 3)
                    sp.dma_start(xT[u][:, :], A["xT"][bass.ds(m, 1)].rearrange("a k n -> k (a n)")).then_inc(s_nxT[u], 16)
                    sp.dma_start(zT[u][:, :], A["zT"][bass.ds(m, 1)].rearrange("a k n -> k (a n)")).then_inc(s_nxT[u], 16)

                def load_x1(g, m, u):
                    wait_count(sp, s_z1, g - 3 - NG)
                    sp.sem_inc(s_sptick, 1)
                    sp.dma_start(x1g[u][:, :, :].rearrange("p t c -> p (t c)"),
                                 x1_rows[bass.ds(m * GROUP, GROUP), :].rearrange("(p t) c -> p (t c)", t=T)).then_inc(s_nxT[u], 32)

                def load_table(g, m, u):
                    if isinstance(m, int) and m == 0:
                        for v in range(2):
                            sp.wait_ge(s_scat[v], (l + 1) * NP * 16)
                    wait_count(sp, s_res, g - 3)
                    sp.sem_inc(s_sptick, 1)
                    sp.dma_start(tab[u][:, :, :].rearrange("p t c -> p (t c)")[:, 0:T * W],
                                 table[l][bass.ds(m * GROUP, GROUP), :].rearrange("(p t) c -> p (t c)", t=T)).then_inc(s_nx[u], 16)

                if l == 0:
                    run_stages(sp, 0, NG, 10, [(0, load_turned), (2, load_table)])
                    sp.dma_start(table[1][N_PAD:ROWS, :].rearrange("(p t) c -> p (t c)", p=P),
                                 zeros[:, 0:2 * LAYERS[1]["ROW"]]).then_inc(s_zero[1], 16)
                else:
                    for u in range(4):
                        sp.wait_ge(s_store[u], stored(NG, u))
                    run_stages(sp, NG, NG, 10, [(0, load_x1), (2, load_table)])
            for u in range(4):
                sp.wait_ge(s_store[u], stored(2 * NG, u))

        @block.gpsimd
        def _(pool):
            nc.gpsimd.memset(ident[:, :], 0.0)
            nc.gpsimd.memset(earlier[:, :], 1.0)
            nc.gpsimd.memset(minus_half[:, :], -0.5)
            nc.gpsimd.memset(quarter[:, :], 0.25)
            nc.gpsimd.iota(spare_i[:, :, :], pattern=[[0, NP], [P, 2]], base=N_PAD, channel_multiplier=1).then_inc(s_step, 1)
            pool.wait_ge(s_step, 1)
            nc.gpsimd.affine_select(out=ident[:, :], in_=ident[:, :], compare_op=ALU.not_equal, fill=1.0,
                                    base=0, pattern=[[-1, P]], channel_multiplier=1)
            nc.gpsimd.affine_select(out=earlier[:, P:PAIR], in_=earlier[:, P:PAIR], compare_op=ALU.is_gt, fill=0.0,
                                    base=0, pattern=[[-1, P]], channel_multiplier=1)
            nc.gpsimd.tensor_copy(spare_row[:, :, :], spare_i[:, :, :]).then_inc(s_pconst, 1)
            for l in range(2):
                rows, width = (A["x_rows"], D + 1) if l == 0 else (x1_rows, D)

                def gather(j, m, u):
                    wait_count(pool, s_xgT, j - 3)
                    if l == 0:
                        wait_count(pool, s_ea, j - 3)
                    pool.wait_ge(s_src[u], landed(j, u, 4))
                    pool.sem_inc(s_ptick, 1)
                    for t in range(2):
                        pool.indirect_dma_start(
                            out=xg[u][:, t, 0:width], out_offset=None, in_=rows,
                            in_offset=bass.IndirectOffsetOnAxis(ap=src_i[u][:, t:t + 1], axis=0)).then_inc(s_gather[u], 16)

                def scatter(j, m, u):
                    wait_count(pool, s_sumsb, j + 1)
                    wait_count(pool, s_row, j + 1)
                    wait_count(pool, s_scat[(u + 1) % 2], landed(j - 1, (u + 1) % 2, 2, 32))
                    if isinstance(j, int) and j == l * NP:
                        pool.wait_ge(s_zero[l], 16 * (25 if l == 0 else NG + 1))
                    pool.sem_inc(s_ptick, 1)
                    W = LAYERS[l]["ROW"]
                    for t in range(2):
                        pool.indirect_dma_start(
                            out=table[l], out_offset=bass.IndirectOffsetOnAxis(ap=row_i[u][:, t:t + 1], axis=0),
                            in_=sums[u][:, t, 0:W], in_offset=None, compute_op=ALU.add).then_inc(s_scat[u], 16)

                if l == 1:
                    for u in range(4):
                        pool.wait_ge(s_store[u], stored(NG, u))
                run_stages(pool, l * NP, NP, 10, [(0, gather), (7, scatter)])

                def powers(g, m, u):
                    st = stats[u]
                    tt, ts = nc.gpsimd.tensor_tensor, nc.gpsimd.tensor_scalar
                    pool.wait_ge(s_bn, g + 1)
                    wait_count(pool, s_y, g - 3)
                    tt(mean2[:, :], st[:, :, 1], st[:, :, 4], ALU.add)
                    tt(apart[:, :], st[:, :, 1], st[:, :, 4], ALU.subtract)
                    tt(squares[:, :], st[:, :, 2], st[:, :, 5], ALU.add).then_inc(s_p1, 1)
                    pool.wait_ge(s_p1, g + 1)
                    tt(apart2[:, :], apart[:, :], apart[:, :], ALU.mult)
                    ts(neg_mean[:, :], mean2[:, :], -0.5, None, ALU.mult)
                    ts(var_in[:, :], squares[:, :], 1.0 / D, EPS, ALU.mult, ALU.add).then_inc(s_p2, 1)
                    pool.wait_ge(s_p2, g + 1)
                    tt(apart2[:, :], apart2[:, :], quarter[:, :], ALU.mult).then_inc(s_p3, 1)
                    pool.wait_ge(s_p3, g + 1)
                    tt(var_e[:, :], var_in[:, :], apart2[:, :], ALU.add).then_inc(s_p4, 1)
                    pool.wait_ge(s_p4, g + 1)
                    tt(rstd[u][:, :], var_e[:, :], minus_half[:, :], ALU.pow).then_inc(s_rstd, 1)
                    pool.wait_ge(s_rstd, g + 1)
                    tt(shift[u][:, :], neg_mean[:, :], rstd[u][:, :], ALU.mult).then_inc(s_shift, 1)

                def factor(g, m, u):
                    tt = nc.gpsimd.tensor_tensor
                    tb, q = tab1[u], small[u]
                    pool.wait_ge(s_q2, g + 1 - NG)
                    a_of = a_all[:, bass.ds(m, 1), :].rearrange("p g t -> p (g t)")
                    tt(q[:, :, 1], a_of, q[:, :, 1], ALU.mult).then_inc(s_q3, 1)
                    pool.wait_ge(s_q3, g + 1 - NG)
                    tt(q[:, :, 2], q[:, :, 1], tb[:, :, 0], ALU.mult).then_inc(s_q4, 1)
                    pool.wait_ge(s_q4, g + 1 - NG)
                    tt(q[:, :, 3], q[:, :, 2], q[:, :, 1], ALU.mult).then_inc(s_q5, 1)

                def scale_gates(g, m, u):
                    pool.wait_ge(s_gate, g + 1)
                    a = a_all[:, bass.ds(m, 1), :].rearrange("p g t -> p (g t)").unsqueeze(2).to_broadcast([P, T, 96])
                    nc.gpsimd.tensor_tensor(gate[u][:, :, :], gate[u][:, :, :], a, ALU.mult).then_inc(s_scgate, 1)

                if l == 0:
                    run_stages(pool, 0, NG, 10, [(0, scale_gates), (3, powers)])
                else:
                    run_stages(pool, NG, NG, 6, [(0, factor), (1, powers)])

        @block.tensor
        def _(pe):
            mm, turn = nc.tensor.matmul, nc.tensor.transpose
            pe.wait_ge(s_scaled, 1)
            pe.wait_ge(s_pconst, 1)
            for l in range(2):
                L = LAYERS[l]
                SO, R2 = L["SO"], 2 * L["R"]

                def turn_x(j, m, u):
                    pe.wait_ge(s_gather[u], landed(j, u, 4, 32))
                    pe.wait_ge(s_xz, j + 1)
                    wait_count(pe, s_xgTsb, j)
                    for t in range(2):
                        turn(xgT_ps[:, t, :], xg[u][:, t, 0:M], ident[:, :])
                    turn(xgT_ps[0:2 * V, 2, :], xz[u][:, :, :], ident[:, :]).then_inc(s_xgT, 1)

                def hidden(j, m, u):
                    pe.wait_ge(s_attr[u], landed(j, u, 4))
                    wait_count(pe, s_hidsb, j)
                    mm(hidT_ps, fc1[l][0:R2, :], attrT[u][0:R2, :], start=True, stop=True).then_inc(s_hid, 1)

                def first_map(j, m, u):
                    pe.wait_ge(s_xgTsb, j + 1)
                    wait_count(pe, s_hs, j)
                    pe.wait_ge(s_hidsb, j + 1)
                    for t in range(2):
                        mm(h_ps[:, t, 0:M], xgT[u][:, t, :], lin1_m[l][:, :], start=True, stop=True)
                    mm(h_ps[:, :, M:D], xgT[u][0:2 * V, 2, :], lin1_z[l][:, :], start=True, stop=True).then_inc(s_h, 1)

                def edge_weights(j, m, u):
                    wait_count(pe, s_mid, j)
                    for t in range(2):
                        q = slice(t * H, (t + 1) * H)
                        last = mm(w_ps[l][:, t, :], hidT[u][q, :], fc2[l][q, :], start=True, stop=True)
                    last.then_inc(s_wd, 1)

                def turn_mid(j, m, u):
                    pe.wait_ge(s_mid, j + 1)
                    wait_count(pe, s_midTsb, j)
                    for c in range(2):
                        for t in range(2):
                            last = turn(midT_ps[:, 2 * c + t, :], mid[u][:, t, c * P:(c + 1) * P], ident[:, :])
                    if L["cross"]:
                        for t in range(2):
                            last = turn(midT_ps[0:96, 4 + t, :], mid[u][:, t, 256:352], ident[:, :])
                    last.then_inc(s_midT, 1)

                def second_map(j, m, u):
                    pe.wait_ge(s_midTsb, j + 1)
                    wait_count(pe, s_ms, j)
                    wait_count(pe, s_mv, j)
                    for t in range(2):
                        mm(o_ps[l][:, t, 0:SO + V], midT[u][:, t, :], mapA[l][:, :], start=t == 0, stop=not L["cross"],
                           skip_group_check=True)
                        last = mm(o_ps[l][:, t, SO + V:SO + 4 * V], midT[u][:, 2 + t, :], mapB[l][:, :], start=False,
                                  stop=not L["cross"], skip_group_check=True)
                        if L["cross"]:
                            last = mm(o_ps[l][:, t, SO:SO + 3 * V], midT[u][0:96, 4 + t, :], mapC[:, :], start=False,
                                      stop=True, skip_group_check=True)
                    last.then_inc(s_o, 1)

                def sum_pair(j, m, u):
                    pe.wait_ge(s_ms, j + 1)
                    pe.wait_ge(s_mv, j + 1)
                    pe.wait_ge(s_same, j + 1)
                    wait_count(pe, s_sumsb, j)
                    mm(sum_ps[l][:, 0, :], same0[u][:, :], msg[l][u][:, 0, :], start=True, stop=False)
                    mm(sum_ps[l][:, 0, :], same1[u][:, 0:P], msg[l][u][:, 1, :], start=False, stop=True)
                    mm(sum_ps[l][:, 1, :], same1[u][:, P:PAIR], msg[l][u][:, 1, :], start=True, stop=True).then_inc(s_sum, 1)

                if l == 1:
                    pe.wait_ge(s_res, NG)
                run_stages(pe, l * NP, NP, 10, [(1, first_map), (0, hidden), (1, edge_weights), (0, turn_x),
                                                (3, second_map), (2, turn_mid), (5, sum_pair)])

                def self_connection(o, z, u, w_m, w_z):
                    for t in range(T):
                        mm(o[:, t // 2, t % 2, 0:z], xT[u][:, t * P:(t + 1) * P], w_m[:, :], start=True, stop=True)
                    for b in range(2):
                        last = mm(o[:, b, :, z:z + V], zT[u][:, :], w_z[:, b * 2 * V:(b + 1) * 2 * V], start=True, stop=True)
                    last.then_inc(s_np, 1)

                def nodes0(g, m, u):
                    pe.wait_ge(s_nxT[u], landed(g, u, 4, 32))
                    wait_count(pe, s_added, g - 1)
                    self_connection(n0_ps[u], 160, u, self_m[0], self_z[0])

                def turn_back(g, m, u):
                    wait_count(pe, s_res, g - 1)
                    for t in range(T):
                        turn(x0_ps[u][:, t, :], xT[u][:, t * P:(t + 1) * P], ident[:, :])
                    turn(z0_ps[u].rearrange("p t c -> p (t c)"), zT[u][:, :], ident[:, :]).then_inc(s_xb, 1)

                def turn1(g, m, u):
                    pe.wait_ge(s_nxT[u], landed(g, u, 4, 32))
                    pe.wait_ge(s_xz, g + 1 + 2 * NP - NG)
                    wait_count(pe, s_nTsb, g - 1 - NG)
                    for t in range(T):
                        turn(x1T_ps[u][:, t * P:(t + 1) * P], x1g[u][:, t, 0:M], ident[:, :])
                    turn(z1T_ps[u], x1z[u][:, :, :], ident[:, :]).then_inc(s_nT, 1)

                def nodes1(g, m, u):
                    pe.wait_ge(s_nTsb, g + 1 - NG)
                    wait_count(pe, s_z1, g - 1 - NG)
                    self_connection(n1_ps[u], M, u, self_m[1], self_z[1])

                pe.wait_ge(s_sumsb, (l + 1) * NP)
                for _ in range(WARM[l]):
                    mm(ps[:, 0:512], ident[:, :], zeros[:, 0:512], start=True, stop=True)
                if l == 0:
                    run_stages(pe, 0, NG, 6, [(0, nodes0), (1, turn_back)])
                else:
                    run_stages(pe, NG, NG, 6, [(0, turn1), (1, nodes1)])

        @block.scalar
        def _(act):
            copy = nc.scalar.copy
            act.wait_ge(s_w, 16 * len(loads))
            W0 = LAYERS[0]["ROW"]
            for k in range(25):
                n = min(2048, ROWS - k * 2048)
                act.dma_start(table[0][k * 2048:k * 2048 + n, :].rearrange("(p r) c -> p (r c)", p=P),
                              zeros[:, 0:n // P * W0]).then_inc(s_zero[0], 16)
            for l in range(2):
                L = LAYERS[l]
                SO, W = L["SO"], L["ROW"]

                def copy_h(j, m, u):
                    act.wait_ge(s_h, j + 1)
                    if not (isinstance(j, int) and j == (l + 1) * NP - 1):
                        act.wait_ge(s_hid, j + 2)
                    wait_count(act, s_mid, j - 1)
                    copy(hs[u][:, :, 0:D], h_ps[:, :, :])
                    copy(hs[u][:, :, D:D + 2 * V], h_ps[:, :, S:S + 2 * V]).then_inc(s_hs, 1)

                def hidden_act(j, m, u):
                    act.wait_ge(s_hid, j + 1)
                    wait_count(act, s_wd, j - 1)
                    nc.scalar.activation(hidT[u][:, :], hidT_ps, ACT.Silu).then_inc(s_hidsb, 1)

                def copy_z(j, m, u):
                    act.wait_ge(s_gather[u], landed(j, u, 4, 32))
                    wait_count(act, s_xgT, j - 1)
                    copy(xz[u][:, :, :], xg[u][:, :, M:D]).then_inc(s_xz, 1)

                def copy_xT(j, m, u):
                    act.wait_ge(s_xgT, j + 1)
                    wait_count(act, s_h, j - 1)
                    copy(xgT[u][:, 0:2, :], xgT_ps[:, 0:2, :])
                    copy(xgT[u][0:2 * V, 2, :], xgT_ps[0:2 * V, 2, :]).then_inc(s_xgTsb, 1)

                def copy_message(j, m, u):
                    act.wait_ge(s_o, j + 1)
                    wait_count(act, s_sum, j - 1)
                    copy(msg[l][u][:, :, 0:SO], o_ps[l][:, :, 0:SO]).then_inc(s_ms, 1)

                def copy_midT(j, m, u):
                    act.wait_ge(s_midT, j + 1)
                    wait_count(act, s_o, j - 1)
                    last = copy(midT[u][:, 0:4, :], midT_ps[:, 0:4, :])
                    if L["cross"]:
                        last = copy(midT[u][0:96, 4:6, :], midT_ps[0:96, 4:6, :])
                    last.then_inc(s_midTsb, 1)

                def copy_sums(j, m, u):
                    act.wait_ge(s_sum, j + 1)
                    wait_count(act, s_scat[u], landed(j - 2, u % 2, 2, 32))
                    copy(sums[u][:, :, 0:W], sum_ps[l][:, :, :]).then_inc(s_sumsb, 1)

                run_stages(act, l * NP, NP, 10, [(0, copy_z), (1, copy_h), (0, hidden_act), (0, copy_xT),
                                                 (3, copy_message), (2, copy_midT), (5, copy_sums)])

                def gates(g, m, u):
                    act.wait_ge(s_added, g + 1)
                    wait_count(act, s_f, g - 1)
                    for t in range(T):
                        a = a_all[:, bass.ds(m, 1), t:t + 1].rearrange("p g t -> p (g t)")
                        last = nc.scalar.activation(gate[u][:, t, :], tab[u][:, t, 0:96], ACT.Sigmoid, scale=a)
                    last.then_inc(s_gate, 1)

                def copy_z1(g, m, u):
                    act.wait_ge(s_nxT[u], landed(g, u, 4, 32))
                    wait_count(act, s_nT, g - 1 - NG)
                    copy(x1z[u][:, :, :], x1g[u][:, :, M:D]).then_inc(s_xz, 1)

                def copy_nT(g, m, u):
                    act.wait_ge(s_nT, g + 1 - NG)
                    wait_count(act, s_np, g - 1)
                    copy(xT[u][:, :], x1T_ps[u])
                    copy(zT[u][:, :], z1T_ps[u]).then_inc(s_nTsb, 1)

                def normalise(g, m, u):
                    act.wait_ge(s_shift, g + 1)
                    wait_count(act, s_store[u], landed(g - 4, u, 4))
                    for t in range(T):
                        last = nc.scalar.activation(y[u][:, t, :], res[u][:, t, :], ACT.Identity,
                                                    scale=rstd[u][:, t:t + 1], bias=shift[u][:, t:t + 1])
                    last.then_inc(s_y, 1)

                def store(g, m, u):
                    act.wait_ge(s_y, g + 1)
                    act.sem_inc(s_atick, 1)
                    to = x1_rows if l == 0 else out
                    act.dma_start(to[bass.ds(m * GROUP, GROUP), :].rearrange("(p t) c -> p (t c)", t=T),
                                  y[u][:, :, :].rearrange("p t c -> p (t c)")).then_inc(s_store[u], 16)

                run_stages(act, l * NG, NG, 10, ([(0, gates)] if l == 0 else [(0, copy_z1), (1, copy_nT)]) + [(5, store), (4, normalise)])

        @block.vector
        def _(dve):
            tt, stt = nc.vector.tensor_tensor, nc.vector.scalar_tensor_tensor
            for w in cleared:
                nc.vector.memset(w[:, :], 0.0)
            for u in range(2):
                nc.vector.memset(msg[1][u][:, :, 161:162], 1.0)
            nc.vector.memset(zeros[:, :], 0.0).then_inc(s_fill, 1)
            dve.wait_ge(s_w, 16 * len(loads))
            dve.wait_ge(s_fill, 1)
            for w, f in scales:
                last = nc.vector.tensor_scalar(w, w, f, None, ALU.mult)
            last.then_inc(s_scaled, 1)
            dve.wait_ge(s_all, 48)
            dve.wait_ge(s_pconst, 1)
            nc.vector.tensor_copy(dst_f[:, :], dst_all[:, :]).then_inc(s_dstf, 1)
            dve.wait_ge(s_dstf, 1)
            tt(to_spare[:, :], spare_row[:, :, :].rearrange("p j t -> p (j t)"), dst_f[:, :], ALU.subtract).then_inc(s_tsp, 1)
            dve.wait_ge(s_tsp, 1)

            def planes(ap):
                return ap.rearrange("p t (i c) -> p t i c", c=V)

            for l in range(2):
                L = LAYERS[l]
                SO = L["SO"]

                def scale_attr(j, m, u):
                    dve.wait_ge(s_gather[u], landed(j, u, 4, 32))
                    at = bass.ds(m * 2, 2)
                    a = xg[u][:, :, D:D + 1].to_broadcast([P, 2, 6])
                    tt(ea_all[:, at, :], attr_all[:, at, :], a, ALU.mult).then_inc(s_ea, 1)

                def products(j, m, u):
                    dve.wait_ge(s_hs, j + 1)
                    if l == 0:
                        dve.wait_ge(s_ea, j + 1)
                    wait_count(dve, s_midT, j - 1)
                    h, w, o = hs[u], w_ps[l], mid[u]
                    hv = h[:, :, S:D + 2 * V].rearrange("p t (i c) -> p t i c", c=V)

                    def comp(k):
                        return ea_all[:, bass.ds(m * 2, 2), k:k + 3].unsqueeze(3).to_broadcast([P, 2, 3, V])

                    def e0(t):
                        return ea_all[:, bass.ds(m * 2 + t, 1), 0:1].rearrange("p a b -> p (a b)")

                    tt(planes(prod[u][:, :, :]), hv[:, :, 0:3, :], comp(1), ALU.mult).then_inc(s_prod, 1)
                    if L["cross"]:
                        tt(planes(crossA[u][:, :, :]), hv[:, :, 1:4, :], comp(3), ALU.mult)
                        tt(planes(crossB[u][:, :, :]), hv[:, :, 2:5, :], comp(2), ALU.mult)
                    dve.wait_ge(s_prod, j + 1)
                    last = tt(dot[u][:, :, :], prod[u][:, :, 0:V], prod[u][:, :, V:2 * V], ALU.add)
                    last.then_inc(s_dot1, 1)
                    dve.wait_ge(s_wd, j + 1)
                    tt(o[:, :, 192:256], h[:, :, 0:S], w[:, :, 64:128], ALU.mult)
                    for t in range(2):
                        stt(o[:, t, 0:S], h[:, t, 0:S], e0(t), w[:, t, 0:S], ALU.mult, ALU.mult)
                    dve.wait_ge(s_dot1, j + 1)
                    tt(dot[u][:, :, :], dot[u][:, :, :], prod[u][:, :, 2 * V:3 * V], ALU.add).then_inc(s_dot2, 1)
                    if L["cross"]:
                        tt(crossA[u][:, :, :], crossA[u][:, :, :], crossB[u][:, :, :], ALU.subtract).then_inc(s_cross, 1)
                    for t in range(2):
                        stt(o[:, t, 96:192].rearrange("p (i c) -> p i c", c=V), hv[:, t, 0:3, :], e0(t),
                            w[:, t:t + 1, 128:160].to_broadcast([P, 3, V]), ALU.mult, ALU.mult)
                    dve.wait_ge(s_dot2, j + 1)
                    last = tt(o[:, :, S:S + V], dot[u][:, :, :], w[:, :, 160:192], ALU.mult)
                    if L["cross"]:
                        dve.wait_ge(s_cross, j + 1)
                        last = tt(planes(o[:, :, 256:352]), planes(crossA[u][:, :, :]),
                                  w[:, :, 192:224].unsqueeze(2).to_broadcast([P, 2, 3, V]), ALU.mult)
                    last.then_inc(s_mid, 1)

                def message_vectors(j, m, u):
                    dve.wait_ge(s_ms, j + 1)
                    wait_count(dve, s_sum, j - 1)
                    e1 = ea_all[:, bass.ds(m * 2, 2), 1:4].unsqueeze(3).to_broadcast([P, 2, 3, V])
                    p32 = o_ps[l][:, :, SO + 3 * V:SO + 4 * V].unsqueeze(2).to_broadcast([P, 2, 3, V])
                    tt(planes(pe1[u][:, :, :]), p32, e1, ALU.mult).then_inc(s_pe1, 1)

                def message_sum(j, m, u):
                    dve.wait_ge(s_pe1, j + 1)
                    tt(msg[l][u][:, :, SO:SO + 3 * V], pe1[u][:, :, :], o_ps[l][:, :, SO:SO + 3 * V], ALU.add).then_inc(s_mv, 1)

                def compare(j, m, u):
                    dve.wait_ge(s_drow[u], landed(j, u, 4))
                    wait_count(dve, s_sum, j - 1)

                    def dst(t):
                        return dst_f[:, bass.ds(m * 2 + t, 1)]

                    nc.vector.tensor_scalar(same0[u][:, :], dst_row[u][:, 0:P], dst(0), None, ALU.is_equal)
                    nc.vector.tensor_scalar(same1[u][:, :], dst_row[u][:, :], dst(1), None, ALU.is_equal).then_inc(s_same, 1)

                def mark_later(j, m, u):
                    dve.wait_ge(s_same, j + 1)
                    dve.sem_inc(s_dtick, 1)
                    ttr = nc.vector.tensor_tensor_reduce
                    ttr(out=junk[:, 0:P], in0=same0[u][:, :], in1=earlier[:, P:PAIR], scale=1.0, scalar=0.0,
                        op0=ALU.mult, op1=ALU.max, accum_out=is_later[u][:, 0:1])
                    ttr(out=junk[:, P:], in0=same1[u][:, :], in1=earlier[:, :], scale=1.0, scalar=0.0,
                        op0=ALU.mult, op1=ALU.max, accum_out=is_later[u][:, 1:2]).then_inc(s_later, 1)

                def step_rows(j, m, u):
                    dve.wait_ge(s_later, j + 1)
                    tt(step[u][:, :], is_later[u][:, :], to_spare[:, bass.ds(m * 2, 2)], ALU.mult).then_inc(s_stepd, 1)

                def choose_rows(j, m, u):
                    wait_count(dve, s_scat[u], landed(j - 2, u % 2, 2, 32))
                    at = bass.ds(m * 2, 2)
                    if l == 0:
                        dve.wait_ge(s_stepd, j + 1)
                        tt(row_i[u][:, :], step[u][:, :], dst_f[:, at], ALU.add)
                        tt(row_all[:, at], step[u][:, :], dst_f[:, at], ALU.add).then_inc(s_row, 1)
                    else:
                        nc.vector.tensor_copy(row_i[u][:, :], row_all[:, at]).then_inc(s_row, 1)

                if l == 0:
                    run_stages(dve, 0, NP, 10, [
                        (4, message_vectors), (0, scale_attr), (4, compare), (4, message_sum), (4, mark_later),
                        (1, products), (4, step_rows), (5, choose_rows)])
                else:
                    run_stages(dve, NP, NP, 10, [
                        (4, message_vectors), (4, compare), (4, message_sum), (1, products), (5, choose_rows)])

                def add_table(g, m, u):
                    dve.wait_ge(s_np, g + 1)
                    dve.wait_ge(s_nx[u], landed(g, u, 4))
                    t4 = tab[u][:, :, :].rearrange("p (b t) c -> p b t c", b=2)
                    tt(t4, n0_ps[u], t4, ALU.add).then_inc(s_added, 1)

                def gated0(g, m, u):
                    dve.wait_ge(s_scgate, g + 1)
                    wait_count(dve, s_y, g - 3)
                    tt(res[u][:, :, 0:S], tab[u][:, :, 0:S], gate[u][:, :, 0:S], ALU.mult)
                    tt(planes(res[u][:, :, S:D]), planes(tab[u][:, :, 96:192]),
                       gate[u][:, :, S:96].unsqueeze(2).to_broadcast([P, T, 3, V]), ALU.mult).then_inc(s_f, 1)

                def residual0(g, m, u):
                    dve.wait_ge(s_f, g + 1)
                    dve.wait_ge(s_xb, g + 1)
                    tt(res[u][:, :, 0:M], res[u][:, :, 0:M], x0_ps[u], ALU.add)
                    tt(res[u][:, :, M:D], res[u][:, :, M:D], z0_ps[u], ALU.add).then_inc(s_res, 1)

                def residual1(g, m, u):
                    tb, q = tab1[u], small[u]
                    dve.wait_ge(s_nx[u], landed(g, u, 4))
                    wait_count(dve, s_res, g - 1)
                    nc.vector.tensor_scalar(q[:, :, 0], tb[:, :, 161], 1.0, None, ALU.max).then_inc(s_q1, 1)
                    dve.wait_ge(s_np, g + 1)
                    wait_count(dve, s_y, g - 3)

                    def self_connection(t):
                        a = a_all[:, bass.ds(m, 1), t:t + 1].rearrange("p g t -> p (g t)")
                        return stt(res[u][:, t, :], n1_ps[u][:, t // 2, t % 2, :], a, x1g[u][:, t, :], ALU.mult, ALU.add)

                    self_connection(0)
                    dve.wait_ge(s_q1, g + 1 - NG)
                    nc.vector.reciprocal(q[:, :, 1], q[:, :, 0]).then_inc(s_q2, 1)
                    for t in range(1, T):
                        last = self_connection(t)
                    last.then_inc(s_z1, 1)

                def table_row1(g, m, u):
                    dve.wait_ge(s_z1, g + 1 - NG)
                    dve.wait_ge(s_q5, g + 1 - NG)
                    for t in range(T):
                        last = stt(res[u][:, t, :], tab1[u][:, t, 1:161], small[u][:, t, 3:4], res[u][:, t, :], ALU.mult, ALU.add)
                    last.then_inc(s_res, 1)

                def stats_of(g, m, u):
                    dve.wait_ge(s_res, g + 1)
                    wait_count(dve, s_shift, g - 1)
                    for t in range(T):
                        last = nc.vector.bn_stats(stats[u][:, t, :], res[u][:, t, :])
                    last.then_inc(s_bn, 1)

                if l == 0:
                    run_stages(dve, 0, NG, 6, [(2, gated0), (0, add_table), (2, residual0), (3, stats_of)])
                else:
                    run_stages(dve, NG, NG, 6, [(0, residual1), (1, stats_of), (0, table_row1)])


_WEIGHTS = [
    "L0_gnn_lin1_ws", "L0_gnn_lin1_wv", "L0_gnn_fc_w1", "L0_gnn_fc_w2", "L0_gnn_sc_ws", "L0_gnn_sc_wv",
    "L0_gnn_lin2_ws", "L0_gnn_lin2_wv", "L1_gnn_Wfc1", "L1_gnn_Wfc2", "L1_gnn_Wsc0", "L1_gnn_Wsc1",
    "L1_gnn_Wl1_0", "L1_gnn_Wl1_1", "L1_gnn_Wl2_s", "L1_gnn_Wl2_v", "L1_gnn_Wa"]


def kernel(**inputs):
    import concourse.bacc as bacc
    from concourse.bass_utils import run_bass_kernel_spmd

    g = {k: np.asarray(v) for k, v in inputs.items()}
    x, a = g["x"], g["node_vec1"]
    planar = np.concatenate([x[:, :S], x[:, S:].reshape(N, V, 3).transpose(0, 2, 1).reshape(N, 3 * V)], 1)
    padded = np.zeros((N_PAD, D), x.dtype)
    padded[:N] = planar
    turned = padded.reshape(NG, P, T, D).transpose(0, 3, 2, 1).reshape(NG, D, GROUP)
    a_node = np.zeros(N_PAD, a.dtype)
    a_node[:N] = a[:, 0]

    def edges(v, fill=0):
        p = np.full((NP * PAIR,) + v.shape[1:], fill, v.dtype)
        p[:E] = v
        return p.reshape((NP, 2, P) + v.shape[1:])

    src, dst = edges(g["src"]), edges(g["dst"], N)
    attr = edges(g["edge_attr_4"])[..., [0, 1, 2, 3, 1, 2]]
    arrays = {
        "x_rows": np.concatenate([planar, a], 1),
        "xT": turned[:, :M], "zT": turned[:, M:].reshape(NG, V, T, P).transpose(0, 2, 1, 3).reshape(NG, T * V, P),
        "a_node": a_node.reshape(NG, P, T).transpose(1, 0, 2).reshape(P, NG * T),
        "src_col": src.transpose(0, 2, 1),
        "dst_col": dst.transpose(2, 0, 1).reshape(P, NP * 2),
        "dst_row": dst.reshape(NP, PAIR),
        "attr6": attr.transpose(2, 0, 1, 3).reshape(P, NP * 12),
        "attrT0": edges(g["edge_attr_64"]).transpose(0, 1, 3, 2).reshape(NP, 128, P),
        "attrT1": edges(g["edge_attr_16"]).transpose(0, 1, 3, 2).reshape(NP, 32, P),
        **{k: g[k] for k in _WEIGHTS},
    }
    arrays = {f"in_{k}": np.ascontiguousarray(v) for k, v in arrays.items()}
    nc = bacc.Bacc("TRN2", target_bir_lowering=False, num_devices=1)
    aps = {k[3:]: nc.dram_tensor(k, v.shape, mybir.dt.from_np(v.dtype), kind="ExternalInput").ap()
           for k, v in arrays.items()}
    out = nc.dram_tensor("out_rows", (N_PAD, D), F32, kind="ExternalOutput").ap()
    program(nc, aps, out)
    r = run_bass_kernel_spmd(nc, [arrays], core_ids=[0]).results[0]["out_rows"]
    r = np.asarray(r)[:N]
    return np.concatenate([r[:, :S], r[:, S:].reshape(N, 3, V).transpose(0, 2, 1).reshape(N, 3 * V)], 1)
```
